# Optimizing a Trainium2 kernel written in Bass

```python
import numpy as np
import jax
import jax.numpy as jnp

def _softmax(x, axis=-1):
    return jax.nn.softmax(x, axis=axis)

def _gelu(x):
    return jax.nn.gelu(x, approximate=True)

def _silu(x):
    return jax.nn.silu(x)

def _sigmoid(x):
    return jax.nn.sigmoid(x)

def _layernorm(x, axis=-1, eps=1e-05):
    m = jnp.mean(x, axis=axis, keepdims=True)
    v = jnp.var(x, axis=axis, keepdims=True)
    return (x - m) / jnp.sqrt(v + eps)

def _scatter_add(tgt, idx, src, axis=0):
    return tgt.at[idx].add(src)

def _segment_sum(src, seg, n):
    return jax.ops.segment_sum(src, seg, n)
kernel_name = 'mk_dlrm_tower_d1_rec_r8_b48892'

def setup_inputs(seed: int=0):
    np.random.seed(seed)
    _w = jnp.asarray

    def _rec_inputs():
        import jax
        import jax.numpy as jnp
        _tk = jax.random.key(seed)
        ids = jnp.stack([jax.random.randint(jax.random.fold_in(_tk, 200 + f), (2048,), 0, v, jnp.int32) for f, v in enumerate([1000, 1000, 12500, 1250, 12500, 1250, 125000, 1000, 1000, 1250, 1000, 1250, 1000, 1000, 1000, 1250, 1000, 1000, 12500, 12500, 1000, 12500, 1000, 12500, 1250, 12500])], axis=1)
        tbl_0 = 0.05 * jax.random.normal(jax.random.fold_in(_tk, 500 + 0), (1000, 128), jnp.float32)
        tbl_1 = 0.05 * jax.random.normal(jax.random.fold_in(_tk, 500 + 1), (1000, 128), jnp.float32)
        tbl_2 = 0.05 * jax.random.normal(jax.random.fold_in(_tk, 500 + 2), (12500, 128), jnp.float32)
        tbl_3 = 0.05 * jax.random.normal(jax.random.fold_in(_tk, 500 + 3), (1250, 128), jnp.float32)
        tbl_4 = 0.05 * jax.random.normal(jax.random.fold_in(_tk, 500 + 4), (12500, 128), jnp.float32)
        tbl_5 = 0.05 * jax.random.normal(jax.random.fold_in(_tk, 500 + 5), (1250, 128), jnp.float32)
        tbl_6 = 0.05 * jax.random.normal(jax.random.fold_in(_tk, 500 + 6), (125000, 128), jnp.float32)
        tbl_7 = 0.05 * jax.random.normal(jax.random.fold_in(_tk, 500 + 7), (1000, 128), jnp.float32)
        tbl_8 = 0.05 * jax.random.normal(jax.random.fold_in(_tk, 500 + 8), (1000, 128), jnp.float32)
        tbl_9 = 0.05 * jax.random.normal(jax.random.fold_in(_tk, 500 + 9), (1250, 128), jnp.float32)
        tbl_10 = 0.05 * jax.random.normal(jax.random.fold_in(_tk, 500 + 10), (1000, 128), jnp.float32)
        tbl_11 = 0.05 * jax.random.normal(jax.random.fold_in(_tk, 500 + 11), (1250, 128), jnp.float32)
        tbl_12 = 0.05 * jax.random.normal(jax.random.fold_in(_tk, 500 + 12), (1000, 128), jnp.float32)
        tbl_13 = 0.05 * jax.random.normal(jax.random.fold_in(_tk, 500 + 13), (1000, 128), jnp.float32)
        tbl_14 = 0.05 * jax.random.normal(jax.random.fold_in(_tk, 500 + 14), (1000, 128), jnp.float32)
        tbl_15 = 0.05 * jax.random.normal(jax.random.fold_in(_tk, 500 + 15), (1250, 128), jnp.float32)
        tbl_16 = 0.05 * jax.random.normal(jax.random.fold_in(_tk, 500 + 16), (1000, 128), jnp.float32)
        tbl_17 = 0.05 * jax.random.normal(jax.random.fold_in(_tk, 500 + 17), (1000, 128), jnp.float32)
        tbl_18 = 0.05 * jax.random.normal(jax.random.fold_in(_tk, 500 + 18), (12500, 128), jnp.float32)
        tbl_19 = 0.05 * jax.random.normal(jax.random.fold_in(_tk, 500 + 19), (12500, 128), jnp.float32)
        tbl_20 = 0.05 * jax.random.normal(jax.random.fold_in(_tk, 500 + 20), (1000, 128), jnp.float32)
        tbl_21 = 0.05 * jax.random.normal(jax.random.fold_in(_tk, 500 + 21), (12500, 128), jnp.float32)
        tbl_22 = 0.05 * jax.random.normal(jax.random.fold_in(_tk, 500 + 22), (1000, 128), jnp.float32)
        tbl_23 = 0.05 * jax.random.normal(jax.random.fold_in(_tk, 500 + 23), (12500, 128), jnp.float32)
        tbl_24 = 0.05 * jax.random.normal(jax.random.fold_in(_tk, 500 + 24), (1250, 128), jnp.float32)
        tbl_25 = 0.05 * jax.random.normal(jax.random.fold_in(_tk, 500 + 25), (12500, 128), jnp.float32)
        _rk = jax.random.fold_in(_tk, 7)
        r_dense_features = -0.000292821 + 1.00034 * jax.random.normal(jax.random.fold_in(_rk, 101), (2048, 128), jnp.float32)
        W_top1 = 0.0405887 * jax.random.normal(jax.random.fold_in(_tk, 801), (607, 512), jnp.float32)
        W_top2 = 0.0441942 * jax.random.normal(jax.random.fold_in(_tk, 802), (512, 256), jnp.float32)
        W_top3 = 0.0625 * jax.random.normal(jax.random.fold_in(_tk, 803), (256, 1), jnp.float32)
        b_top1 = jnp.zeros((512,), jnp.float32)
        b_top2 = jnp.zeros((256,), jnp.float32)
        return (r_dense_features, ids, tbl_0, tbl_1, tbl_2, tbl_3, tbl_4, tbl_5, tbl_6, tbl_7, tbl_8, tbl_9, tbl_10, tbl_11, tbl_12, tbl_13, tbl_14, tbl_15, tbl_16, tbl_17, tbl_18, tbl_19, tbl_20, tbl_21, tbl_22, tbl_23, tbl_24, tbl_25, W_top1, b_top1, W_top2, b_top2, W_top3)
    r_dense_features, ids, tbl_0, tbl_1, tbl_2, tbl_3, tbl_4, tbl_5, tbl_6, tbl_7, tbl_8, tbl_9, tbl_10, tbl_11, tbl_12, tbl_13, tbl_14, tbl_15, tbl_16, tbl_17, tbl_18, tbl_19, tbl_20, tbl_21, tbl_22, tbl_23, tbl_24, tbl_25, W_top1, b_top1, W_top2, b_top2, W_top3 = _rec_inputs()

    def _L0_rec_setup():
        import jax, jax.numpy as jnp
        import numpy as np
        F = 26
        _TRIU_I, _TRIU_J = np.triu_indices(F + 1, k=1)
        key = jax.random.key(seed)
        k1, k2 = jax.random.split(key)
        B, D = (4096, 128)
        dense_features = jax.random.normal(k1, (B, D), dtype=jnp.float32)
        sparse_features = jax.random.normal(k2, (B, F, D), dtype=jnp.float32)
        return {'dense_features': dense_features, 'sparse_features': sparse_features}
    _L0_rec_all = _L0_rec_setup()
    _L0_rec_in = {k: v for k, v in _L0_rec_all.items() if k in ()}
    del _L0_rec_all
    return {'r_dense_features': r_dense_features, 'ids': ids, 'tbl_0': tbl_0, 'tbl_1': tbl_1, 'tbl_2': tbl_2, 'tbl_3': tbl_3, 'tbl_4': tbl_4, 'tbl_5': tbl_5, 'tbl_6': tbl_6, 'tbl_7': tbl_7, 'tbl_8': tbl_8, 'tbl_9': tbl_9, 'tbl_10': tbl_10, 'tbl_11': tbl_11, 'tbl_12': tbl_12, 'tbl_13': tbl_13, 'tbl_14': tbl_14, 'tbl_15': tbl_15, 'tbl_16': tbl_16, 'tbl_17': tbl_17, 'tbl_18': tbl_18, 'tbl_19': tbl_19, 'tbl_20': tbl_20, 'tbl_21': tbl_21, 'tbl_22': tbl_22, 'tbl_23': tbl_23, 'tbl_24': tbl_24, 'tbl_25': tbl_25, 'W_top1': W_top1, 'b_top1': b_top1, 'W_top2': W_top2, 'b_top2': b_top2, 'W_top3': W_top3}

def reference(r_dense_features, ids, tbl_0, tbl_1, tbl_2, tbl_3, tbl_4, tbl_5, tbl_6, tbl_7, tbl_8, tbl_9, tbl_10, tbl_11, tbl_12, tbl_13, tbl_14, tbl_15, tbl_16, tbl_17, tbl_18, tbl_19, tbl_20, tbl_21, tbl_22, tbl_23, tbl_24, tbl_25, W_top1, b_top1, W_top2, b_top2, W_top3):
    import jax
    import jax.numpy as jnp

    def _L0_rec_ref(dense_features, sparse_features):
        import jax, jax.numpy as jnp
        import numpy as np
        F = 26
        _TRIU_I, _TRIU_J = np.triu_indices(F + 1, k=1)
        combined = jnp.concatenate([dense_features[:, None, :], sparse_features], axis=1)
        interactions = jnp.einsum('bfd,bgd->bfg', combined, combined)
        interactions_flat = interactions[:, _TRIU_I, _TRIU_J]
        return jnp.concatenate([dense_features, interactions_flat], axis=1)
    e = jnp.stack([tbl_0[ids[:, 0]], tbl_1[ids[:, 1]], tbl_2[ids[:, 2]], tbl_3[ids[:, 3]], tbl_4[ids[:, 4]], tbl_5[ids[:, 5]], tbl_6[ids[:, 6]], tbl_7[ids[:, 7]], tbl_8[ids[:, 8]], tbl_9[ids[:, 9]], tbl_10[ids[:, 10]], tbl_11[ids[:, 11]], tbl_12[ids[:, 12]], tbl_13[ids[:, 13]], tbl_14[ids[:, 14]], tbl_15[ids[:, 15]], tbl_16[ids[:, 16]], tbl_17[ids[:, 17]], tbl_18[ids[:, 18]], tbl_19[ids[:, 19]], tbl_20[ids[:, 20]], tbl_21[ids[:, 21]], tbl_22[ids[:, 22]], tbl_23[ids[:, 23]], tbl_24[ids[:, 24]], tbl_25[ids[:, 25]]], axis=1)
    z = _L0_rec_ref(r_dense_features, e)
    z = z.reshape(z.shape[0], -1)
    h = jnp.concatenate([z, r_dense_features], axis=1)
    h = jnp.maximum(h @ W_top1 + b_top1, 0.0)
    h = jnp.maximum(h @ W_top2 + b_top2, 0.0)
    y = h @ W_top3
    return y

_drawn_inputs = setup_inputs


def setup_inputs(seed=0):
    import zlib

    import numpy as np

    out = dict(_drawn_inputs(seed))
    spreads = {'b_top1': (0.0, 0.1), 'b_top2': (0.0, 0.1)}
    factors = {}
    for name, (base, spread) in spreads.items():
        noise = np.random.default_rng([zlib.crc32(name.encode()), seed]).standard_normal(out[name].shape)
        drawn = base * np.exp(spread * noise) if base else spread * noise
        out[name] = jnp.asarray(drawn.astype(out[name].dtype))
    for name, factor in factors.items():
        out[name] = (out[name] * factor).astype(out[name].dtype)
    return out
```

```python
from contextlib import ExitStack

import concourse.bass as bass
from concourse import mybir

F32 = mybir.dt.float32
F16 = mybir.dt.float16
BF16 = mybir.dt.bfloat16
I32 = mybir.dt.int32
ALU = mybir.AluOpType
ACT = mybir.ActivationFunctionType

P = 128
BATCH, D = 2048, 128
VOCAB = [1000, 1000, 12500, 1250, 12500, 1250, 125000, 1000, 1000, 1250, 1000, 1250, 1000,
         1000, 1000, 1250, 1000, 1000, 12500, 12500, 1000, 12500, 1000, 12500, 1250, 12500]
H1, H2 = 512, 256

SLOTS = len(VOCAB) + 1
COLS = SLOTS - 1
PAIRS = SLOTS * COLS // 2
PAIR_START = [c * COLS - c * (c - 1) // 2 for c in range(COLS)]

PICKED = [7, 8, 10, 12, 14, 16, 17]
NX = len(PICKED)
ROWS = 1000
VP, VQ = 125, ROWS // 125
assert all(VOCAB[f] == ROWS for f in PICKED)
PARTS = 3

BATCHES = [(0, 1), (4, 1), (10, 2), (19, 1), (23, 1)]
NB = len(BATCHES)
ARRIVING = [s + k * step for s, step in BATCHES for k in range(4)]
NG = len(ARRIVING) - 1
assert sorted(ARRIVING + [f + 1 for f in PICKED]) == list(range(SLOTS))

TILES = BATCH // P
TP = 4
PHASES = TILES // TP
NS = TP * P
GT = P // 4
GROUPS = TP * GT
PITCH = 32
KZ = PAIRS // 3
M1, M2 = H1 // P, H2 // P

U_Z, U_ZT, U_H1, U_H2, U_Y = 0, 7, 10, 14, 16
USES = 17
EMPTIED = ((USES + 1) // 2, USES // 2)
CHUNKS = [range(0, 4), range(4, 7), range(7, 10), range(10, 12), range(12, 14), range(14, 16),
          range(16, 17)]
assert len(CHUNKS) <= NX


def evens(k):
    return (k + 1) // 2


def odds(k):
    return k // 2


def dlrm_tower(nc, dense, ids, tables, w1_in, b1_in, w2_in, b2_in, w3_in, out):
    with ExitStack() as ctx:
        def sb(name, shape, dt):
            return ctx.enter_context(nc.sbuf_tensor(name, shape, dt))

        def psum(name, shape):
            return ctx.enter_context(nc.psum_tensor(name, shape, F32))

        def sem(name):
            return ctx.enter_context(nc.semaphore(name))

        ident = sb("ident", [P, P], F32)
        ident16 = sb("ident16", [P, P], F16)
        vocab_i = sb("vocab_i", [P, VQ], I32)
        vocab_f = sb("vocab_f", [P, VQ], F32)
        ids_all = sb("ids_all", [P, TILES, len(VOCAB)], I32)
        ids16 = sb("ids16", [P, NX, TILES], F16)
        ids_phase = sb("ids_phase", [P, NX, TP], F16)
        ids_tile = sb("ids_tile", [P, TP, len(VOCAB)], I32)
        arrived = sb("arrived", [P, TP, NB * 4, D], F32)
        cols = sb("cols", [P, TP, P, PITCH], F32)
        prod = sb("prod", [P, COLS, GROUPS], F32)
        pairs = sb("pairs", [P, 4, PAIRS], F32)
        pairs_t = sb("pairs_t", [P, 3, NS], F32)
        dense_t = sb("dense_t", [P, NS], F32)
        ids_wide = sb("ids_wide", [P, 2, NS], F16)
        onehot = sb("onehot", [P, 2, VQ, NS], BF16)
        table = sb("table", [P, NX, PARTS, VQ * D], BF16)
        w1 = sb("w1", [P, 4, M1, P], F32)
        w2 = sb("w2", [P, M1, M2, P], F32)
        w3 = sb("w3", [P, M2], F32)
        b1 = sb("b1", [P, M1], F32)
        b2 = sb("b2", [P, M2], F32)
        y_all = sb("y_all", [P, TILES], F32)

        spare = prod[:].rearrange("p c g -> p (c g)")
        h1 = spare[:, 0:M1 * NS].rearrange("p (m s) -> p m s", m=M1)
        h2 = spare[:, M1 * NS:(M1 + M2) * NS].rearrange("p (m s) -> p m s", m=M2)
        w1_raw = spare[:, 0:5 * H1].rearrange("p (k h) -> p k h", k=5)
        w2_raw = pairs_t[:].rearrange("p k s -> p (k s)")[:, 0:M1 * H2].rearrange("p (m h) -> p m h", m=M1)
        table_raw = arrived[:, TP - 1, 0:2 * VQ, :].rearrange("p (i q) d -> p i (q d)", i=2)
        rest = pairs[:].rearrange("p j k -> p (j k)")[:, 0:VQ * D]

        ps_ids = psum("ps_ids", [P, NS])
        ps_pick = psum("ps_pick", [P, NS])
        ps_tr = psum("ps_tr", [P, 2, 4 * P])
        ps_prod = psum("ps_prod", [P, 4, 4, P])

        s_raw = [sem("s_raw0"), sem("s_raw1")]
        s_hi = sem("s_hi")
        s_rest = sem("s_rest")
        s_mid = sem("s_mid")
        s_lo = sem("s_lo")
        s_ids = sem("s_ids")
        s_ids16 = sem("s_ids16")
        s_ident = sem("s_ident")
        s_ident0 = sem("s_ident0")
        s_const = sem("s_const")
        s_w_raw = sem("s_w_raw")
        s_w = sem("s_w")
        s_phase = sem("s_phase")
        s_idt = [sem(f"s_idt{t}") for t in range(TP)]
        s_dense = [sem(f"s_dense{t}") for t in range(TP)]
        s_rows = [sem(f"s_rows{t}") for t in range(TP)]
        s_wide_ps = sem("s_wide_ps")
        s_wide = sem("s_wide")
        s_onehot = sem("s_onehot")
        s_pick = sem("s_pick")
        s_picked = sem("s_picked")
        s_tr = sem("s_tr")
        s_cols = [sem("s_cols_v"), sem("s_cols_s")]
        s_prod_ps = sem("s_prod_ps")
        s_prod = [sem("s_prod_v"), sem("s_prod_s")]
        s_dense_t = sem("s_dense_t")
        s_tail_ps = sem("s_tail_ps")
        s_tail = [sem("s_tail_v"), sem("s_tail_s")]
        s_turn = sem("s_turn")
        s_out = sem("s_out")

        ids_rows = ids.rearrange("(p t) f -> p t f", t=TILES)
        dense_rows = dense.rearrange("(p t) d -> p t d", t=TILES)

        def batch_columns(t, b):
            s0, step = BATCHES[b]
            return cols[:, t, :, s0:s0 + 3 * step + 1:step].rearrange("d p s -> d s p")


        def empty_batch(copy, t, b, done):
            k = t * NB + b
            copy(batch_columns(t, b), ps_tr[:, k % 2, :].rearrange("d (s p) -> d s p", s=4)).then_inc(done, 1)

        def empty_products(copy, t, h, done):
            b = 2 * (h % 2)
            g = t * GT + 8 * h
            for j in range(4):
                at = slice(32 * j, 32 * j + 32)
                for_j = ps_prod[at, b:b + 2, :, j * COLS:(j + 1) * COLS].rearrange("r b g c -> r (b g) c")
                last = copy(prod[at, :, g:g + 8].rearrange("r c g -> r g c"), for_j)
            last.then_inc(done, 1)

        def empty_pairs(copy, u, done):
            bank = ps_prod[:, u % 4].rearrange("g c (j r) -> g c j r", j=4)
            for c in range(4 * u, min(4 * u + 4, COLS)):
                start, n = PAIR_START[c], COLS - c
                last = copy(pairs[:, :, start:start + n], bank[:, c % 4, :, c + 1:SLOTS])
            last.then_inc(done, 1)

        def empty_pairs_t(copy, u, done):
            bank = ps_prod[0:KZ, u % 4]
            copy(pairs_t[0:KZ, u - U_ZT, :].rearrange("k (g j) -> k j g", j=4), bank).then_inc(done, 1)

        block = ctx.enter_context(nc.Block())

        @block.sync
        def _(sp):
            sp.dma_start(ids_all[:], ids_rows).then_inc(s_ids, 16)

            def load_tile(n, t, first):
                if not first:
                    sp.wait_ge(s_rows[t], 16 * NG * n)
                sp.dma_start(ids_tile[:, t, :], ids_rows[:, n * TP + t, :]).then_inc(s_idt[t], 16)
                if not first:
                    sp.wait_ge(s_tr, (n - 1) * TP * NB + (t + 1) * NB)
                elif t == TP - 1:
                    sp.wait_ge(s_lo, NX)
                sp.dma_start(arrived[:, t, 0, :], dense_rows[:, n * TP + t, :]).then_inc(s_dense[t], 16)

            load_tile(0, 0, True)
            for i in range(NX):
                if i >= 2:
                    sp.wait_ge(s_rest, i - 1)
                sp.dma_start(table_raw[0:VP, i % 2, :],
                             tables[PICKED[i]].rearrange("(p q) d -> p (q d)", q=VQ)).then_inc(s_raw[i % 2], 16)
                if i < TP - 2:
                    load_tile(0, i + 1, True)
                if i == 3:
                    sp.dma_start(w1_raw[:, 0, :], w1_in[0:D, :]).then_inc(s_w_raw, 16)
                    sp.dma_start(w1_raw[:, 1, :], w1_in[D + PAIRS:, :]).then_inc(s_w_raw, 16)
                    sp.dma_start(w1_raw[0:KZ, 2:5, :],
                                 w1_in[D:D + PAIRS, :].rearrange("(k p) h -> p k h", p=KZ)).then_inc(s_w_raw, 16)
                    sp.dma_start(w2_raw, w2_in.rearrange("(p m) h -> p m h", m=M1)).then_inc(s_w_raw, 16)
                    sp.dma_start(w3[:], w3_in.rearrange("(p m) o -> p (m o)", m=M2)).then_inc(s_w_raw, 16)
                    sp.dma_start(b1[:], b1_in.rearrange("(p m) -> p m", m=M1)).then_inc(s_w_raw, 16)
                    sp.dma_start(b2[:], b2_in.rearrange("(p m) -> p m", m=M2)).then_inc(s_w_raw, 16)
            load_tile(0, TP - 1, True)
            with sp.Fori(1, PHASES) as n:
                for t in range(TP):
                    load_tile(n, t, False)
            sp.wait_ge(s_tail[0], PHASES * EMPTIED[0])
            sp.dma_start(out.rearrange("(p t) o -> p (t o)", t=TILES), y_all[:]).then_inc(s_out, 16)
            sp.wait_ge(s_out, 16)

        @block.gpsimd
        def _(pool):
            nc.gpsimd.memset(ident[:], 0.0).then_inc(s_ident0, 1)
            pool.wait_ge(s_ident0, 1)
            nc.gpsimd.affine_select(out=ident[:], in_=ident[:], compare_op=ALU.not_equal, fill=1.0, base=0,
                                    pattern=[[-1, P]], channel_multiplier=1).then_inc(s_ident, 1)
            nc.gpsimd.iota(vocab_i[:], pattern=[[1, VQ]], base=0, channel_multiplier=VQ).then_inc(s_ident, 1)

            def gather_tile(n, t, first):
                pool.wait_ge(s_idt[t], 16 * (n + 1))
                if first and t == TP - 1:
                    pool.wait_ge(s_lo, NX)
                if not first:
                    pool.wait_ge(s_tr, (n - 1) * TP * NB + (t + 1) * NB)
                    pool.sem_inc(s_turn, 1)
                for k in range(1, NG + 1):
                    f = ARRIVING[k] - 1
                    pool.indirect_dma_start(arrived[:, t, k, :], None, tables[f],
                                            bass.IndirectOffsetOnAxis(ids_tile[:, t, f:f + 1], 0)
                                            ).then_inc(s_rows[t], 16)

            for t in range(TP):
                gather_tile(0, t, True)
            with pool.Fori(1, PHASES) as n:
                for t in range(TP):
                    gather_tile(n, t, False)

        @block.tensor
        def _(pe):
            def spread_ids(n, i, first):
                if i == 0:
                    pe.wait_ge(s_phase, n + 1)
                if not (first and i == 0):
                    pe.wait_ge(s_wide, n * NX + i)
                for t in range(TP):
                    last = nc.tensor.matmul(ps_ids[:, t * P:(t + 1) * P],
                                            ids_phase[:, i, t:t + 1].to_broadcast([P, P]), ident16[:],
                                            start=True, stop=True)
                last.then_inc(s_wide_ps, 1)

            def pick_rows(n, i, first):
                pe.wait_ge(s_onehot, (n * NX + i + 1) * VQ)
                if not (first and i == 0):
                    pe.wait_ge(s_picked, n * NX + i)
                if first:
                    pe.wait_ge(s_lo, i + 1)
                for q in range(VQ):
                    for part in range(PARTS):
                        last = nc.tensor.matmul(ps_pick[:], table[0:VP, i, part, q * D:(q + 1) * D],
                                                onehot[0:VP, i % 2, q, :],
                                                start=(q == 0 and part == 0), stop=(q == VQ - 1 and part == PARTS - 1))
                last.then_inc(s_pick, 1)

            def transpose_tile(n, t):
                pe.wait_ge(s_rows[t], 16 * NG * (n + 1))
                pe.wait_ge(s_dense[t], 16 * (n + 1))
                for b in range(NB):
                    k = t * NB + b
                    if not (isinstance(n, int) and n == 0 and k < 2):
                        pe.wait_ge(s_cols[k % 2], n * (TP * NB // 2) + k // 2)
                    for s in range(4):
                        last = nc.tensor.transpose(ps_tr[:, k % 2, s * P:(s + 1) * P],
                                                   arrived[:, t, 4 * b + s, :], ident[:])
                    last.then_inc(s_tr, 1)

            def multiply_tile(n, t, first):
                pe.wait_ge(s_cols[0], n * (TP * NB // 2) + evens((t + 1) * NB))
                pe.wait_ge(s_cols[1], n * (TP * NB // 2) + odds((t + 1) * NB))
                if t == 0:
                    pe.wait_ge(s_picked, (n + 1) * NX)
                    if not first:
                        pe.wait_ge(s_tail[0], n * EMPTIED[0])
                        pe.wait_ge(s_tail[1], n * EMPTIED[1])
                for h in range(4):
                    if not (first and t == 0 and h < 2):
                        pe.wait_ge(s_prod[h % 2], (n * TP + t) * 2 + h // 2)
                    for g in range(8):
                        s = 4 * (8 * h + g)
                        dst = ps_prod[:, 2 * (h % 2) + g // 4, g % 4, 0:4 * COLS]
                        last = nc.tensor.matmul(dst, cols[:, t, s:s + 4, :].rearrange("d p s -> d (p s)"),
                                                cols[:, t, s:s + 4, 0:COLS],
                                                start=True, stop=True)
                    last.then_inc(s_prod_ps, 1)

            def tail(n, chunk, first):
                for u in CHUNKS[chunk]:
                    e, even, odd = u % 4, n * EMPTIED[0], n * EMPTIED[1]
                    if u >= 4:
                        pe.wait_ge(s_tail[u % 2], (odd if u % 2 else even) + u // 2 - 1)
                    if u == U_Z:
                        pe.wait_ge(s_prod[0], (n + 1) * TP * 2)
                        pe.wait_ge(s_prod[1], (n + 1) * TP * 2)
                    if u in (U_ZT, U_H1, U_H2, U_Y):
                        pe.wait_ge(s_tail[0], even + evens(u))
                        pe.wait_ge(s_tail[1], odd + odds(u))
                    if u == U_H1:
                        pe.wait_ge(s_dense_t, n + 1)
                        if first:
                            pe.wait_ge(s_w, 9)
                    if u < U_ZT:
                        for c in range(4 * u, min(4 * u + 4, COLS)):
                            last = nc.tensor.transpose(ps_prod[:, e, c % 4, :], prod[:, c, :], ident[:])
                    elif u < U_H1:
                        k = u - U_ZT
                        for j in range(4):
                            last = nc.tensor.transpose(ps_prod[0:KZ, e, j, :], pairs[:, j, k * KZ:(k + 1) * KZ],
                                                       ident[:])
                    elif u < U_H2:
                        m = u - U_H1
                        dst = ps_prod[:, e].rearrange("p g c -> p (g c)")
                        nc.tensor.matmul(dst, w1[:, 0, m, :], dense_t[:], start=True, stop=False)
                        for k in range(3):
                            last = nc.tensor.matmul(dst, w1[0:KZ, k + 1, m, :], pairs_t[0:KZ, k, :],
                                                    start=False, stop=(k == 2))
                    elif u < U_Y:
                        m = u - U_H2
                        dst = ps_prod[:, e].rearrange("p g c -> p (g c)")
                        for k in range(M1):
                            last = nc.tensor.matmul(dst, w2[:, k, m, :], h1[:, k, :],
                                                    start=(k == 0), stop=(k == M1 - 1))
                    else:
                        for t in range(TP):
                            for k in range(M2):
                                last = nc.tensor.matmul(ps_prod[:, e, 0, t:t + 1], h2[:, k, t * P:(t + 1) * P],
                                                        w3[:, k:k + 1], start=(k == 0), stop=(k == M2 - 1))
                    last.then_inc(s_tail_ps, 1)

            def phase(n, first):
                spread_ids(n, 0, first)
                for i in range(NX):
                    if i + 1 < NX:
                        spread_ids(n, i + 1, first)
                    if not first and i < len(CHUNKS):
                        tail(n - 1, i, False)
                    pick_rows(n, i, first)
                transpose_tile(n, 0)
                for t in range(TP):
                    if t + 1 < TP:
                        transpose_tile(n, t + 1)
                    multiply_tile(n, t, first)

            pe.wait_ge(s_const, 2)
            phase(0, True)
            pe.wait_ge(s_w, 9)
            with pe.Fori(1, PHASES) as n:
                phase(n, False)
            for chunk in range(len(CHUNKS)):
                tail(PHASES - 1, chunk, False)

        @block.vector
        def _(dve):
            copy = nc.vector.tensor_copy

            def one_hot(n, i, first):
                for q in range(VQ):
                    if q == 0:
                        dve.wait_ge(s_wide, n * NX + i + 1)
                        if not (first and i < 2):
                            dve.wait_ge(s_pick, n * NX + i - 1)
                    nc.vector.tensor_scalar(onehot[0:VP, i % 2, q, :], ids_wide[0:VP, i % 2, :],
                                            vocab_f[0:VP, q:q + 1], None, ALU.is_equal).then_inc(s_onehot, 1)

            def split_table(i):
                raw = table_raw[0:VP, i % 2, :]
                dve.wait_ge(s_hi, i + 1)
                if i:
                    dve.wait_ge(s_mid, i)
                    dve.wait_ge(s_lo, i)
                nc.vector.tensor_tensor(rest[0:VP], raw, table[0:VP, i, 0, :], ALU.subtract).then_inc(s_rest, 1)
                dve.wait_ge(s_mid, i + 1)
                dve.wait_ge(s_rest, i + 1)
                nc.vector.tensor_tensor(table[0:VP, i, 2, :], rest[0:VP], table[0:VP, i, 1, :],
                                        ALU.subtract).then_inc(s_lo, 1)

            def lay_out_weights():
                dve.wait_ge(s_w_raw, 16 * 7)
                nc.vector.tensor_tensor(w1[:, 0, :, :].rearrange("p m j -> p j m"),
                                        w1_raw[:, 0, :].rearrange("p (j m) -> p j m", m=M1),
                                        w1_raw[:, 1, :].rearrange("p (j m) -> p j m", m=M1), ALU.add).then_inc(s_w, 1)
                for k in range(3):
                    nc.vector.tensor_copy(w1[0:KZ, k + 1, :, :].rearrange("p m j -> p j m"),
                                          w1_raw[0:KZ, k + 2, :].rearrange("p (j m) -> p j m", m=M1)).then_inc(s_w, 1)
                for k in range(M1):
                    nc.vector.tensor_copy(w2[:, k, :, :].rearrange("p m j -> p j m"),
                                          w2_raw[:, k, :].rearrange("p (j m) -> p j m", m=M2)).then_inc(s_w, 1)
                dve.wait_ge(s_lo, NX)
                nc.vector.memset(cols[:, :, :, SLOTS:PITCH], 0.0).then_inc(s_w, 1)

            def empty_tile(n, t):
                for b in range(NB):
                    if (t * NB + b) % 2 == 0:
                        dve.wait_ge(s_tr, n * TP * NB + t * NB + b + 1)
                        empty_batch(copy, t, b, s_cols[0])

            def empty_tail(n, chunk):
                for u in CHUNKS[chunk]:
                    if u % 2:
                        continue
                    dve.wait_ge(s_tail_ps, n * USES + u + 1)
                    bank = ps_prod[:, u % 4].rearrange("p g c -> p (g c)")
                    if u < U_ZT:
                        empty_pairs(copy, u, s_tail[0])
                    elif u < U_H1:
                        empty_pairs_t(copy, u, s_tail[0])
                    elif u < U_H2:
                        m = u - U_H1
                        nc.vector.tensor_scalar(h1[:, m, :], bank, b1[:, m:m + 1], 0.0, ALU.add,
                                                ALU.max).then_inc(s_tail[0], 1)
                    elif u < U_Y:
                        m = u - U_H2
                        nc.vector.tensor_scalar(h2[:, m, :], bank, b2[:, m:m + 1], 0.0, ALU.add,
                                                ALU.max).then_inc(s_tail[0], 1)
                    else:
                        copy(y_all[:, bass.ds(n * TP, TP)], bank[:, 0:TP]).then_inc(s_tail[0], 1)

            def phase(n, first):
                if not first:
                    dve.wait_ge(s_wide_ps, n * NX)
                copy(ids_phase[:], ids16[:, :, bass.ds(n * TP, TP)]).then_inc(s_phase, 1)
                if first:
                    split_table(0)
                one_hot(n, 0, first)
                for i in range(NX):
                    if first and i + 1 < NX:
                        split_table(i + 1)
                    if not first and i < len(CHUNKS):
                        empty_tail(n - 1, i)
                    if i + 1 < NX:
                        one_hot(n, i + 1, first)
                if first:
                    lay_out_weights()
                empty_tile(n, 0)
                for t in range(TP):
                    if t + 1 < TP:
                        empty_tile(n, t + 1)
                    for h in (0, 2):
                        dve.wait_ge(s_prod_ps, n * TP * 4 + 4 * t + h + 1)
                        empty_products(copy, t, h, s_prod[0])

            dve.wait_ge(s_ident, 2)
            copy(ident16[:], ident[:]).then_inc(s_const, 1)
            copy(vocab_f[:], vocab_i[:]).then_inc(s_const, 1)
            dve.wait_ge(s_ids, 16)
            for i, f in enumerate(PICKED):
                copy(ids16[:, i, :], ids_all[:, :, f]).then_inc(s_ids16, 1)
            dve.wait_ge(s_ids16, NX)
            dve.wait_ge(s_const, 2)
            phase(0, True)
            with dve.Fori(1, PHASES) as n:
                phase(n, False)
            for chunk in range(len(CHUNKS)):
                empty_tail(PHASES - 1, chunk)

        @block.scalar
        def _(act):
            copy = nc.scalar.copy

            def widen(n, i, first):
                act.wait_ge(s_wide_ps, n * NX + i + 1)
                if not (first and i < 2):
                    act.wait_ge(s_onehot, (n * NX + i - 1) * VQ)
                copy(ids_wide[:, i % 2, :], ps_ids[:]).then_inc(s_wide, 1)

            def split_table(i):
                act.wait_ge(s_raw[i % 2], 16 * (i // 2 + 1))
                copy(table[0:VP, i, 0, :], table_raw[0:VP, i % 2, :]).then_inc(s_hi, 1)
                act.wait_ge(s_rest, i + 1)
                copy(table[0:VP, i, 1, :], rest[0:VP]).then_inc(s_mid, 1)

            def empty_tile(n, t):
                for b in range(NB):
                    if (t * NB + b) % 2:
                        act.wait_ge(s_tr, n * TP * NB + t * NB + b + 1)
                        empty_batch(copy, t, b, s_cols[1])

            def empty_tail(n, chunk):
                for u in CHUNKS[chunk]:
                    if u % 2 == 0:
                        continue
                    act.wait_ge(s_tail_ps, n * USES + u + 1)
                    bank = ps_prod[:, u % 4].rearrange("p g c -> p (g c)")
                    if u < U_ZT:
                        empty_pairs(copy, u, s_tail[1])
                    elif u < U_H1:
                        empty_pairs_t(copy, u, s_tail[1])
                    elif u < U_H2:
                        m = u - U_H1
                        nc.scalar.activation(h1[:, m, :], bank, ACT.Relu, bias=b1[:, m:m + 1]).then_inc(s_tail[1], 1)
                    else:
                        m = u - U_H2
                        nc.scalar.activation(h2[:, m, :], bank, ACT.Relu, bias=b2[:, m:m + 1]).then_inc(s_tail[1], 1)

            def phase(n, first):
                if first:
                    split_table(0)
                widen(n, 0, first)
                for i in range(NX):
                    if first and i + 1 < NX:
                        split_table(i + 1)
                    if i + 1 < NX:
                        widen(n, i + 1, first)
                    if not first and i < len(CHUNKS):
                        empty_tail(n - 1, i)
                    act.wait_ge(s_pick, n * NX + i + 1)
                    copy(cols[:, :, :, PICKED[i] + 1], ps_pick[:].rearrange("d (t p) -> d t p", t=TP)
                         ).then_inc(s_picked, 1)
                if first:
                    act.wait_ge(s_w, 9)
                empty_tile(n, 0)
                for t in range(TP):
                    if t + 1 < TP:
                        empty_tile(n, t + 1)
                    for h in (1, 3):
                        act.wait_ge(s_prod_ps, n * TP * 4 + 4 * t + h + 1)
                        empty_products(copy, t, h, s_prod[1])
                act.wait_ge(s_cols[0], (n + 1) * (TP * NB // 2))
                copy(dense_t[:].rearrange("d (t p) -> d t p", t=TP), cols[:, :, :, 0]).then_inc(s_dense_t, 1)

            phase(0, True)
            with act.Fori(1, PHASES) as n:
                phase(n, False)
            for chunk in range(len(CHUNKS)):
                empty_tail(PHASES - 1, chunk)



def kernel(**inputs):
    import numpy as _np
    import concourse.bacc as _bacc
    from concourse import mybir as _mybir
    from concourse.bass_utils import run_bass_kernel_spmd as _run

    nc = _bacc.Bacc("TRN2", target_bir_lowering=False, num_devices=1)
    arrays, args = {}, {}
    names = ["r_dense_features", "ids"] + [f"tbl_{f}" for f in range(len(VOCAB))]
    for name in names + ["W_top1", "b_top1", "W_top2", "b_top2", "W_top3"]:
        a = _np.ascontiguousarray(inputs[name])
        arrays[f"in_{name}_dram"] = a
        args[name] = nc.dram_tensor(f"in_{name}_dram", a.shape, _mybir.dt.from_np(a.dtype), kind="ExternalInput").ap()
    out = nc.dram_tensor("out_0_dram", (BATCH, 1), F32, kind="ExternalOutput").ap()
    dlrm_tower(nc, args["r_dense_features"], args["ids"], [args[f"tbl_{f}"] for f in range(len(VOCAB))],
               args["W_top1"], args["b_top1"], args["W_top2"], args["b_top2"], args["W_top3"], out)
    r = _run(nc, [arrays], core_ids=[0])
    return r.results[0]["out_0_dram"]
```

```python
from contextlib import ExitStack

import concourse.bass as bass
from concourse import mybir

F32 = mybir.dt.float32
F16 = mybir.dt.float16
F32R = mybir.dt.float32r
I32 = mybir.dt.int32
ALU = mybir.AluOpType
ACT = mybir.ActivationFunctionType

P = 128
BATCH, D = 2048, 128
VOCAB = [1000, 1000, 12500, 1250, 12500, 1250, 125000, 1000, 1000, 1250, 1000, 1250, 1000,
         1000, 1000, 1250, 1000, 1000, 12500, 12500, 1000, 12500, 1000, 12500, 1250, 12500]
H1, H2 = 512, 256

SLOTS = len(VOCAB) + 1
COLS = SLOTS - 1
PAIRS = SLOTS * COLS // 2
PAIR_START = [c * COLS - c * (c - 1) // 2 for c in range(COLS)]

PICKED = [7, 8, 10, 12, 14, 16, 17, 22]
NX = len(PICKED)
ROWS = 1000
VP, VQ = 125, ROWS // 125
assert all(VOCAB[f] == ROWS for f in PICKED)
HI, LO = 0, 1

BATCHES = [(0, 1, 4), (4, 1, 4), (10, 2, 4), (19, 1, 4), (24, 1, 3)]
NB = len(BATCHES)
ARRIVING = [s + k * step for s, step, count in BATCHES for k in range(count)]
PLACE = [4 * b for b in range(NB)]
NG = len(ARRIVING) - 1
assert sorted(ARRIVING + [f + 1 for f in PICKED]) == list(range(SLOTS))

TILES = BATCH // P
TP = 2
PHASES = TILES // TP
NS = TP * P
GT = P // 4
GROUPS = TP * GT
PITCH = 32
KZ = PAIRS // 3
M1, M2 = H1 // P, H2 // P

PIECES = NX + 4

U_Z, U_ZT, U_H1, U_H2, U_Y = 0, 4, 6, 8, 9
USES = 10
V, S = 0, 1
EMPTIER = [S, V, S, V, V, V, S, S, S, V]
CHUNKS = [range(0, 4), range(0), range(4, 6), range(6, 7), range(7, 8), range(8, 9), range(9, 10)]
assert len(CHUNKS) <= NX


def emptied(engine, uses):
    return sum(e == engine for e in EMPTIER[:uses])


def dlrm_tower(nc, dense, ids, tables, w1_in, b1_in, w2_in, b2_in, w3_in, out):
    with ExitStack() as ctx:
        def sb(name, shape, dt):
            return ctx.enter_context(nc.sbuf_tensor(name, shape, dt))

        def psum(name, shape):
            return ctx.enter_context(nc.psum_tensor(name, shape, F32))

        def sem(name):
            return ctx.enter_context(nc.semaphore(name))

        ident = sb("ident", [P, P], F32)
        ident16 = sb("ident16", [P, P], F16)
        vocab_i = sb("vocab_i", [P, VQ], I32)
        vocab_f = sb("vocab_f", [P, VQ], F32)
        ids_all = sb("ids_all", [P, TILES, len(VOCAB)], I32)
        ids16 = sb("ids16", [P, NX, TILES], F16)
        ids_phase = sb("ids_phase", [P, NX, TP], F16)
        ids_tile = sb("ids_tile", [P, TP, len(VOCAB)], I32)
        arrived = sb("arrived", [P, TP, NG + 1, D], F32)
        cols = sb("cols", [P, TP, P, PITCH], F32)
        pairs = sb("pairs", [GROUPS, 4, PAIRS], F32)
        ids_wide = sb("ids_wide", [P, 2, NS], F16)
        onehot = sb("onehot", [P, 2, VQ, NS], F32R)
        table = sb("table", [P, NX, 2, VQ * D], F32R)
        h1_full = sb("h1_full", [P, M1, NS], F32)
        h2 = sb("h2", [P, M2, NS], F32)
        w1 = sb("w1", [P, 2, 4, M1, P], F32R)
        w2 = sb("w2", [P, 2, M1, M2, P], F32R)
        with nc.sbuf_tensor("prod", [P, COLS, GROUPS], F32) as prod:
            pass
        h1 = sb("h1", [P, 2, M1, NS], F32R)
        with nc.sbuf_tensor("raw", [P, 2, VQ * D], F32) as raw:
            pass
        pairs_t = sb("pairs_t", [P, 2, 3, NS], F32R)
        dense_t = sb("dense_t", [P, 2, NS], F32R)
        w3 = sb("w3", [P, M2], F32)
        b1 = sb("b1", [P, M1], F32)
        b2 = sb("b2", [P, M2], F32)
        y_all = sb("y_all", [P, TILES], F32)

        ps_ids = psum("ps_ids", [P, NS])
        ps_pick = psum("ps_pick", [P, NS])
        ps_tr = psum("ps_tr", [P, 2, 4 * P])
        ps_prod = psum("ps_prod", [P, 4, 4, P])

        s_raw = [sem("s_raw0"), sem("s_raw1")]
        s_sum = sem("s_sum")
        s_hi = sem("s_hi")
        s_lo = sem("s_lo")
        s_ids = sem("s_ids")
        s_ids16 = sem("s_ids16")
        s_ident = sem("s_ident")
        s_ident0 = sem("s_ident0")
        s_const = sem("s_const")
        s_small = sem("s_small")
        s_zero = sem("s_zero")
        s_phase = sem("s_phase")
        s_idt = [sem(f"s_idt{t}") for t in range(TP)]
        s_dense = [sem(f"s_dense{t}") for t in range(TP)]
        s_rows = [sem(f"s_rows{t}") for t in range(TP)]
        s_wide_ps = sem("s_wide_ps")
        s_wide = sem("s_wide")
        s_onehot = sem("s_onehot")
        s_pick = sem("s_pick")
        s_picked = sem("s_picked")
        s_tr = sem("s_tr")
        s_cols = sem("s_cols")
        s_prod_ps = sem("s_prod_ps")
        s_prod = [sem("s_prod_v"), sem("s_prod_s")]
        s_dense_hi = sem("s_dense_hi")
        s_dense_lo = sem("s_dense_lo")
        s_pairs_hi = sem("s_pairs_hi")
        s_h1_hi = sem("s_h1_hi")
        s_h1_lo = sem("s_h1_lo")
        s_tail_ps = sem("s_tail_ps")
        s_tail = [sem("s_tail_v"), sem("s_tail_s")]
        s_turn = sem("s_turn")
        s_turn_pe = sem("s_turn_pe")
        s_out = sem("s_out")

        ids_rows = ids.rearrange("(p t) f -> p t f", t=TILES)
        dense_rows = dense.rearrange("(p t) d -> p t d", t=TILES)

        def batch_columns(t, b):
            s0, step, count = BATCHES[b]
            return cols[:, t, :, s0:s0 + (count - 1) * step + 1:step].rearrange("d p s -> d s p")


        def empty_products(copy, t, h, done):
            b = 2 * (h % 2)
            g = t * GT + 8 * h
            for j in range(4):
                at = slice(32 * j, 32 * j + 32)
                for_j = ps_prod[at, b:b + 2, :, j * COLS:(j + 1) * COLS].rearrange("r b g c -> r (b g) c")
                last = copy(prod[at, :, g:g + 8].rearrange("r c g -> r g c"), for_j)
            last.then_inc(done, 1)

        def empty_pairs(copy, u, done):
            for c in range(8 * u, min(8 * u + 8, COLS)):
                half = slice(GROUPS * (c % 2), GROUPS * (c % 2) + GROUPS)
                bank = ps_prod[half, u % 4, (c % 8) // 2].rearrange("g (j r) -> g j r", j=4)
                start, n = PAIR_START[c], COLS - c
                last = copy(pairs[:, :, start:start + n], bank[:, :, c + 1:SLOTS])
            last.then_inc(done, 1)

        def pair_rows(u):
            thirds = range(2) if u == U_ZT else range(2, 3)
            bank = ps_prod[0:KZ, u % 4].rearrange("k a b -> k (a b)")[:, 0:len(thirds) * NS]
            return thirds, bank.rearrange("k (z j g) -> k z j g", z=len(thirds), j=4)

        def pair_part(part, thirds):
            dst = pairs_t[0:KZ, part, thirds[0]:thirds[-1] + 1, :]
            return dst.rearrange("k z (g j) -> k z j g", j=4)

        def piece(i):
            buf = raw[:, i % 2, :]
            if i < NX:
                return buf[0:VP], table[0:VP, i, HI, :], table[0:VP, i, LO, :]
            if i < NX + 3:
                k0, count, rows = [(0, 1, P), (1, 2, KZ), (3, 1, KZ)][i - NX]
                src = buf[0:rows, 0:count * H1].rearrange("p (k j m) -> p k m j", k=count, m=M1)
                return src, w1[0:rows, HI, k0:k0 + count], w1[0:rows, LO, k0:k0 + count]
            src = buf.rearrange("p (k j m) -> p k m j", k=M1, m=M2)
            return src, w2[:, HI], w2[:, LO]

        block = ctx.enter_context(nc.Block())

        @block.sync
        def _(sp):
            sp.dma_start(ids_all[:], ids_rows).then_inc(s_ids, 16)

            def load_tile(n, t, first):
                if not first:
                    sp.wait_ge(s_rows[t], 16 * NG * n)
                sp.dma_start(ids_tile[:, t, :], ids_rows[:, bass.ds(n * TP + t, 1), :].rearrange("p a f -> p (a f)")
                             ).then_inc(s_idt[t], 16)
                if not first:
                    sp.wait_ge(s_tr, (n - 1) * TP * NB + (t + 1) * NB)
                sp.dma_start(arrived[:, t, 0, :], dense_rows[:, bass.ds(n * TP + t, 1), :].rearrange("p a d -> p (a d)")
                             ).then_inc(s_dense[t], 16)

            def load_piece(i):
                if i >= 2:
                    sp.wait_ge(s_lo, i - 1)
                buf = raw[:, i % 2, :]
                if i < NX:
                    sp.dma_start(buf[0:VP], tables[PICKED[i]].rearrange("(p q) d -> p (q d)", q=VQ)
                                 ).then_inc(s_raw[i % 2], 16)
                elif i == NX:
                    sp.dma_start(buf[:, 0:H1], w1_in[0:D, :]).then_inc(s_raw[i % 2], 16)
                    sp.dma_start(buf[:, H1:2 * H1], w1_in[D + PAIRS:, :]).then_inc(s_raw[i % 2], 16)
                elif i < NX + 3:
                    k0, count = [(0, 2), (2, 1)][i - NX - 1]
                    sp.dma_start(buf[0:KZ, 0:count * H1].rearrange("p (k h) -> p k h", k=count),
                                 w1_in[D + k0 * KZ:D + (k0 + count) * KZ, :].rearrange("(k p) h -> p k h", p=KZ)
                                 ).then_inc(s_raw[i % 2], 16)
                else:
                    sp.dma_start(buf, w2_in.rearrange("(p m) h -> p (m h)", m=M1)).then_inc(s_raw[i % 2], 16)

            load_tile(0, 0, True)
            load_piece(0)
            load_tile(0, 1, True)
            sp.dma_start(w3[:], w3_in.rearrange("(p m) o -> p (m o)", m=M2)).then_inc(s_small, 16)
            sp.dma_start(b1[:], b1_in.rearrange("(p m) -> p m", m=M1)).then_inc(s_small, 16)
            sp.dma_start(b2[:], b2_in.rearrange("(p m) -> p m", m=M2)).then_inc(s_small, 16)
            for i in range(1, PIECES):
                load_piece(i)
            with sp.Fori(1, PHASES) as n:
                for t in range(TP):
                    load_tile(n, t, False)
            sp.wait_ge(s_tail[V], PHASES * emptied(V, USES))
            sp.dma_start(out.rearrange("(p t) o -> p (t o)", t=TILES), y_all[:]).then_inc(s_out, 16)
            sp.wait_ge(s_out, 16)

        @block.gpsimd
        def _(pool):
            nc.gpsimd.memset(ident[:], 0.0).then_inc(s_ident0, 1)
            pool.wait_ge(s_ident0, 1)
            nc.gpsimd.affine_select(out=ident[:], in_=ident[:], compare_op=ALU.not_equal, fill=1.0, base=0,
                                    pattern=[[-1, P]], channel_multiplier=1).then_inc(s_ident, 1)
            nc.gpsimd.iota(vocab_i[:], pattern=[[1, VQ]], base=0, channel_multiplier=VQ).then_inc(s_ident, 1)

            def gather_tile(n, t, first):
                pool.wait_ge(s_idt[t], 16 * (n + 1))
                if not first:
                    pool.wait_ge(s_tr, (n - 1) * TP * NB + (t + 1) * NB)
                    pool.sem_inc(s_turn, 1)
                for k in range(1, NG + 1):
                    f = ARRIVING[k] - 1
                    pool.indirect_dma_start(arrived[:, t, k, :], None, tables[f],
                                            bass.IndirectOffsetOnAxis(ids_tile[:, t, f:f + 1], 0)
                                            ).then_inc(s_rows[t], 16)

            for t in range(TP):
                gather_tile(0, t, True)
            with pool.Fori(1, PHASES) as n:
                for t in range(TP):
                    gather_tile(n, t, False)

        @block.tensor
        def _(pe):
            def spread_ids(n, i):
                if i == 0:
                    pe.wait_ge(s_phase, n + 1)
                if not (isinstance(n, int) and n == 0 and i == 0):
                    pe.wait_ge(s_wide, n * NX + i)
                for t in range(TP):
                    last = nc.tensor.matmul(ps_ids[:, t * P:(t + 1) * P],
                                            ids_phase[:, i, t:t + 1].to_broadcast([P, P]), ident16[:],
                                            start=True, stop=True)
                last.then_inc(s_wide_ps, 1)

            def pick_rows(n, i, first):
                pe.wait_ge(s_onehot, (n * NX + i + 1) * VQ)
                if not (first and i == 0):
                    pe.wait_ge(s_picked, n * NX + i)
                if first:
                    pe.wait_ge(s_lo, i + 1)
                for q in range(VQ):
                    for part in (HI, LO):
                        last = nc.tensor.matmul(ps_pick[:], table[0:VP, i, part, q * D:(q + 1) * D],
                                                onehot[0:VP, i % 2, q, :],
                                                start=(q == 0 and part == 0), stop=(q == VQ - 1 and part == LO))
                last.then_inc(s_pick, 1)

            def transpose_batch(n, t, b):
                if b == 0:
                    pe.wait_ge(s_rows[t], 16 * NG * (n + 1))
                    pe.wait_ge(s_dense[t], 16 * (n + 1))
                k = t * NB + b
                if not (isinstance(n, int) and n == 0 and k < 2):
                    pe.wait_ge(s_cols, n * TP * NB + k - 1)
                for s in range(BATCHES[b][2]):
                    last = nc.tensor.transpose(ps_tr[:, k % 2, s * P:(s + 1) * P],
                                               arrived[:, t, PLACE[b] + s, :], ident[:])
                last.then_inc(s_tr, 1)

            def multiply_tile(n, t, first):
                pe.wait_ge(s_cols, n * TP * NB + (t + 1) * NB)
                if t == 0:
                    pe.wait_ge(s_picked, (n + 1) * NX)
                    if first:
                        pe.wait_ge(s_zero, 1)
                    else:
                        pe.wait_ge(s_tail[V], n * emptied(V, USES))
                        pe.wait_ge(s_tail[S], n * emptied(S, USES))
                for h in range(4):
                    if not (first and t == 0 and h < 2):
                        pe.wait_ge(s_prod[h % 2], (n * TP + t) * 2 + h // 2)
                    for g in range(8):
                        s = 4 * (8 * h + g)
                        dst = ps_prod[:, 2 * (h % 2) + g // 4, g % 4, 0:4 * COLS]
                        last = nc.tensor.matmul(dst, cols[:, t, s:s + 4, :].rearrange("d p s -> d (p s)"),
                                                cols[:, t, s:s + 4, 0:COLS], start=True, stop=True)
                    last.then_inc(s_prod_ps, 1)
                    if t == 0 and h + 2 < NB:
                        transpose_batch(n, 1, h + 2)

            def layer(dst, weights, inputs):
                parts = [(HI, HI), (HI, LO), (LO, HI)]
                for k, (w, x) in enumerate(zip(weights, inputs)):
                    for a, b in parts:
                        last = nc.tensor.matmul(dst, w[:, a], x[:, b], start=(k == 0 and (a, b) == parts[0]),
                                                stop=(k == len(inputs) - 1 and (a, b) == parts[-1]))
                return last

            def tail(n, chunk):
                base = [n * emptied(e, USES) for e in (V, S)]
                for u in CHUNKS[chunk]:
                    bank = ps_prod[:, u % 4].rearrange("p a b -> p (a b)")
                    if u >= 4:
                        e = EMPTIER[u - 4]
                        pe.wait_ge(s_tail[e], base[e] + emptied(e, u - 3))
                    if u == U_Z:
                        pe.wait_ge(s_prod[0], (n + 1) * TP * 2)
                        pe.wait_ge(s_prod[1], (n + 1) * TP * 2)
                    if u in (U_ZT, U_H1, U_Y):
                        pe.wait_ge(s_tail[V], base[V] + emptied(V, u))
                        pe.wait_ge(s_tail[S], base[S] + emptied(S, u))
                    if U_ZT <= u < U_H1:
                        pe.sem_inc(s_turn_pe, 1)
                    if u == U_H1:
                        pe.wait_ge(s_dense_lo, n + 1)
                    if u == U_H2:
                        pe.wait_ge(s_h1_lo, (n + 1) * M1)
                    if u < U_ZT:
                        for c in range(8 * u, min(8 * u + 8, COLS), 2):
                            last = nc.tensor.transpose(ps_prod[:, u % 4, (c % 8) // 2, :],
                                                       prod[:, c:c + 2, :].rearrange("r c g -> r (c g)"), ident[:])
                    elif u < U_H1:
                        thirds, dst = pair_rows(u)
                        for z, k in enumerate(thirds):
                            for j in range(4):
                                last = nc.tensor.transpose(dst[:, z, j, :], pairs[:, j, k * KZ:(k + 1) * KZ],
                                                           ident[0:GROUPS, 0:GROUPS])
                    elif u < U_H2:
                        for z in range(2):
                            m = 2 * (u - U_H1) + z
                            last = layer(bank[:, z * NS:(z + 1) * NS],
                                         [w1[:, :, 0, m, :]] + [w1[0:KZ, :, k + 1, m, :] for k in range(3)],
                                         [dense_t[:]] + [pairs_t[0:KZ, :, k, :] for k in range(3)])
                    elif u < U_Y:
                        for m in range(M2):
                            last = layer(bank[:, m * NS:(m + 1) * NS],
                                         [w2[:, :, k, m, :] for k in range(M1)], [h1[:, :, k, :] for k in range(M1)])
                    else:
                        for t in range(TP):
                            for k in range(M2):
                                last = nc.tensor.matmul(bank[:, t:t + 1], h2[:, k, t * P:(t + 1) * P],
                                                        w3[:, k:k + 1], start=(k == 0), stop=(k == M2 - 1))
                    last.then_inc(s_tail_ps, 1)

            def picks(n, first):
                for i in range(NX):
                    if i + 2 < NX:
                        spread_ids(n, i + 2)
                    pick_rows(n, i, first)
                    if not first and i < len(CHUNKS):
                        tail(n - 1, i)
                    if NX - 1 - NB <= i < NX - 1:
                        transpose_batch(n, 0, i - (NX - 1 - NB))
                transpose_batch(n, 1, 0)
                transpose_batch(n, 1, 1)

            def tiles(n, first, last):
                if not last:
                    spread_ids(n + 1, 0)
                multiply_tile(n, 0, first)
                if not last:
                    spread_ids(n + 1, 1)
                multiply_tile(n, 1, first)

            pe.wait_ge(s_const, 2)
            spread_ids(0, 0)
            spread_ids(0, 1)
            picks(0, True)
            tiles(0, True, False)
            pe.wait_ge(s_small, 16 * 3)
            pe.wait_ge(s_lo, PIECES)
            picks(1, False)
            with pe.Fori(2, PHASES) as n:
                tiles(n - 1, False, False)
                picks(n, False)
            tiles(PHASES - 1, False, True)
            for chunk in range(len(CHUNKS)):
                tail(PHASES - 1, chunk)

        @block.vector
        def _(dve):
            copy = nc.vector.tensor_copy

            def one_hot(n, i, first):
                for q in range(VQ):
                    if q == 0:
                        dve.wait_ge(s_wide, n * NX + i + 1)
                        if not (first and i < 2):
                            dve.wait_ge(s_pick, n * NX + i - 1)
                    nc.vector.tensor_scalar(onehot[0:VP, i % 2, q, :], ids_wide[0:VP, i % 2, :],
                                            vocab_f[0:VP, q:q + 1], None, ALU.is_equal).then_inc(s_onehot, 1)

            def split_piece(i):
                src, hi, lo = piece(i)
                if i == NX:
                    dve.wait_ge(s_raw[i % 2], 16 * (i // 2 + 2))
                    nc.vector.tensor_tensor(raw[:, i % 2, 0:H1], raw[:, i % 2, 0:H1], raw[:, i % 2, H1:2 * H1],
                                            ALU.add).then_inc(s_sum, 1)
                dve.wait_ge(s_hi, i + 1)
                nc.vector.tensor_tensor(lo, src, hi.bitcast(F32), ALU.subtract).then_inc(s_lo, 1)

            def empty_tail(n, chunk):
                for u in CHUNKS[chunk]:
                    bank = ps_prod[:, u % 4].rearrange("p g c -> p (g c)")
                    if U_H1 <= u < U_H2:
                        for m in range(2 * (u - U_H1), 2 * (u - U_H1) + 2):
                            dve.wait_ge(s_h1_hi, n * M1 + m + 1)
                            nc.vector.tensor_tensor(h1[:, LO, m, :], h1_full[:, m, :], h1[:, HI, m, :].bitcast(F32),
                                                    ALU.subtract).then_inc(s_h1_lo, 1)
                    if EMPTIER[u] != V:
                        continue
                    dve.wait_ge(s_tail_ps, n * USES + u + 1)
                    if u < U_ZT:
                        empty_pairs(copy, u, s_tail[V])
                    elif u < U_H1:
                        thirds, src = pair_rows(u)
                        dve.wait_ge(s_pairs_hi, n * 2 + (u - U_ZT) + 1)
                        for z, k in enumerate(thirds):
                            last = nc.vector.tensor_tensor(pair_part(LO, [k])[:, 0], src[:, z],
                                                           pair_part(HI, [k])[:, 0].bitcast(F32), ALU.subtract)
                        last.then_inc(s_tail[V], 1)
                    else:
                        copy(y_all[:, bass.ds(n * TP, TP)], bank[:, 0:TP]).then_inc(s_tail[V], 1)

            def stage_ids(n):
                if not (isinstance(n, int) and n == 0):
                    dve.wait_ge(s_wide_ps, n * NX)
                copy(ids_phase[:], ids16[:, :, bass.ds(n * TP, TP)]).then_inc(s_phase, 1)

            def picks(n, first):
                for i in range(NX):
                    if first and 0 < i < NX - 1:
                        split_piece(i + 1)
                    if not first and i < len(CHUNKS):
                        empty_tail(n - 1, i)
                    if i + 2 < NX:
                        one_hot(n, i + 2, first)

            def tiles(n, last):
                if not last:
                    stage_ids(n + 1)
                for t in range(TP):
                    for h in (0, 2):
                        dve.wait_ge(s_prod_ps, n * TP * 4 + 4 * t + h + 1)
                        empty_products(copy, t, h, s_prod[0])
                        if isinstance(n, int) and n == 0:
                            split_piece(NX + 2 * t + h // 2)
                        if not last and (t, h) in ((0, 2), (1, 0)):
                            one_hot(n + 1, t, False)
                dve.wait_ge(s_dense_hi, n + 1)
                nc.vector.tensor_tensor(dense_t[:, LO].rearrange("d (t p) -> d t p", t=TP), cols[:, :, :, 0],
                                        dense_t[:, HI].bitcast(F32).rearrange("d (t p) -> d t p", t=TP),
                                        ALU.subtract).then_inc(s_dense_lo, 1)

            dve.wait_ge(s_ident, 2)
            copy(ident16[:], ident[:]).then_inc(s_const, 1)
            nc.vector.memset(cols[:, :, :, SLOTS:PITCH], 0.0).then_inc(s_zero, 1)
            copy(vocab_f[:], vocab_i[:]).then_inc(s_const, 1)
            dve.wait_ge(s_ids, 16)
            for i, f in enumerate(PICKED):
                copy(ids16[:, i, :], ids_all[:, :, f]).then_inc(s_ids16, 1)
            dve.wait_ge(s_ids16, NX)
            dve.wait_ge(s_const, 2)
            dve.wait_ge(s_small, 16 * 3)
            stage_ids(0)
            split_piece(0)
            one_hot(0, 0, True)
            split_piece(1)
            one_hot(0, 1, True)
            picks(0, True)
            tiles(0, False)
            picks(1, False)
            with dve.Fori(2, PHASES) as n:
                tiles(n - 1, False)
                picks(n, False)
            tiles(PHASES - 1, True)
            for chunk in range(len(CHUNKS)):
                empty_tail(PHASES - 1, chunk)

        @block.scalar
        def _(act):
            copy = nc.scalar.copy

            def widen(n, i, first):
                act.wait_ge(s_wide_ps, n * NX + i + 1)
                if not (first and i < 2):
                    act.wait_ge(s_onehot, (n * NX + i - 1) * VQ)
                copy(ids_wide[:, i % 2, :], ps_ids[:]).then_inc(s_wide, 1)

            def split_piece(i):
                src, hi, lo = piece(i)
                if i == NX:
                    act.wait_ge(s_sum, 1)
                else:
                    act.wait_ge(s_raw[i % 2], 16 * (i // 2 + 1 + (i > NX and (i - NX) % 2 == 0)))
                copy(hi, src).then_inc(s_hi, 1)

            def empty_batch(n, t, b):
                k, count = t * NB + b, BATCHES[b][2]
                act.wait_ge(s_tr, n * TP * NB + k + 1)
                if k == 0 and not (isinstance(n, int) and n == 0):
                    act.wait_ge(s_dense_lo, n)
                copy(batch_columns(t, b), ps_tr[:, k % 2, 0:count * P].rearrange("d (s p) -> d s p", s=count)
                     ).then_inc(s_cols, 1)

            def empty_tail(n, chunk):
                for u in CHUNKS[chunk]:
                    bank = ps_prod[:, u % 4].rearrange("p g c -> p (g c)")
                    if U_ZT <= u < U_H1:
                        thirds, src = pair_rows(u)
                        act.wait_ge(s_tail_ps, n * USES + u + 1)
                        for z, k in enumerate(thirds):
                            last = copy(pair_part(HI, [k])[:, 0], src[:, z])
                        last.then_inc(s_pairs_hi, 1)
                    if EMPTIER[u] != S:
                        continue
                    act.wait_ge(s_tail_ps, n * USES + u + 1)
                    if u < U_ZT:
                        empty_pairs(copy, u, s_tail[S])
                    elif u == U_H2:
                        for m in range(M2):
                            last = nc.scalar.activation(h2[:, m, :], bank[:, m * NS:(m + 1) * NS], ACT.Relu,
                                                        bias=b2[:, m:m + 1])
                        last.then_inc(s_tail[S], 1)
                    else:
                        tiles = range(2 * (u - U_H1), 2 * (u - U_H1) + 2)
                        for z, m in enumerate(tiles):
                            last = nc.scalar.activation(h1_full[:, m, :], bank[:, z * NS:(z + 1) * NS], ACT.Relu,
                                                        bias=b1[:, m:m + 1])
                        last.then_inc(s_tail[S], 1)
                        act.wait_ge(s_tail[S], n * emptied(S, USES) + emptied(S, u + 1))
                        for m in tiles:
                            copy(h1[:, HI, m, :], h1_full[:, m, :]).then_inc(s_h1_hi, 1)

            def picks(n, first):
                for i in range(NX):
                    if first and 0 < i < NX - 1:
                        split_piece(i + 1)
                    if i + 2 < NX:
                        widen(n, i + 2, first)
                    act.wait_ge(s_pick, n * NX + i + 1)
                    copy(cols[:, :, :, PICKED[i] + 1], ps_pick[:].rearrange("d (t p) -> d t p", t=TP)
                         ).then_inc(s_picked, 1)
                    if not first and i < len(CHUNKS):
                        empty_tail(n - 1, i)
                    if NX - 1 - NB <= i < NX - 1:
                        empty_batch(n, 0, i - (NX - 1 - NB))
                empty_batch(n, 1, 0)
                empty_batch(n, 1, 1)

            def tiles(n, last):
                for t in range(TP):
                    if not last:
                        widen(n + 1, t, False)
                    for h in range(4):
                        if h % 2:
                            act.wait_ge(s_prod_ps, n * TP * 4 + 4 * t + h + 1)
                            empty_products(copy, t, h, s_prod[1])
                            if isinstance(n, int) and n == 0:
                                split_piece(NX + 2 * t + h // 2)
                        if t == 0 and h + 2 < NB:
                            empty_batch(n, 1, h + 2)
                if isinstance(n, int) and n == 0:
                    act.wait_ge(s_lo, PIECES)
                copy(dense_t[:, HI].rearrange("d (t p) -> d t p", t=TP), cols[:, :, :, 0]).then_inc(s_dense_hi, 1)

            act.wait_ge(s_small, 16 * 3)
            split_piece(0)
            widen(0, 0, True)
            split_piece(1)
            widen(0, 1, True)
            picks(0, True)
            tiles(0, False)
            picks(1, False)
            with act.Fori(2, PHASES) as n:
                tiles(n - 1, False)
                picks(n, False)
            tiles(PHASES - 1, True)
            for chunk in range(len(CHUNKS)):
                empty_tail(PHASES - 1, chunk)



def kernel(**inputs):
    import numpy as _np
    import concourse.bacc as _bacc
    from concourse import mybir as _mybir
    from concourse.bass_utils import run_bass_kernel_spmd as _run

    nc = _bacc.Bacc("TRN2", target_bir_lowering=False, num_devices=1)
    arrays, args = {}, {}
    names = ["r_dense_features", "ids"] + [f"tbl_{f}" for f in range(len(VOCAB))]
    for name in names + ["W_top1", "b_top1", "W_top2", "b_top2", "W_top3"]:
        a = _np.ascontiguousarray(inputs[name])
        arrays[f"in_{name}_dram"] = a
        args[name] = nc.dram_tensor(f"in_{name}_dram", a.shape, _mybir.dt.from_np(a.dtype), kind="ExternalInput").ap()
    out = nc.dram_tensor("out_0_dram", (BATCH, 1), F32, kind="ExternalOutput").ap()
    dlrm_tower(nc, args["r_dense_features"], args["ids"], [args[f"tbl_{f}"] for f in range(len(VOCAB))],
               args["W_top1"], args["b_top1"], args["W_top2"], args["b_top2"], args["W_top3"], out)
    r = _run(nc, [arrays], core_ids=[0])
    return r.results[0]["out_0_dram"]
```

```python
from contextlib import ExitStack

import concourse.bass as bass
from concourse import mybir

F32 = mybir.dt.float32
F16 = mybir.dt.float16
F32R = mybir.dt.float32r
I32 = mybir.dt.int32
ALU = mybir.AluOpType
ACT = mybir.ActivationFunctionType

P = 128
BATCH, D = 2048, 128
VOCAB = [1000, 1000, 12500, 1250, 12500, 1250, 125000, 1000, 1000, 1250, 1000, 1250, 1000,
         1000, 1000, 1250, 1000, 1000, 12500, 12500, 1000, 12500, 1000, 12500, 1250, 12500]
H1, H2 = 512, 256

SLOTS = len(VOCAB) + 1
COLS = SLOTS - 1
PAIRS = SLOTS * COLS // 2
PAIR_START = [c * COLS - c * (c - 1) // 2 for c in range(COLS)]

PICKED = [12, 13, 14, 16, 17, 22]
NX = len(PICKED)
PICKED_AT_START = [7, 8]
NE = len(PICKED_AT_START)
NX0 = NX + NE
ROWS = 1000
VP, VQ = 125, ROWS // 125
assert all(VOCAB[f] == ROWS for f in PICKED + PICKED_AT_START)
HI, LO = 0, 1

BATCHES = [(0, 1, 4), (4, 1, 4), (8, 1, 4), (12, 4, 2), (19, 1, 4), (24, 1, 3)]
NB = len(BATCHES)
HB = NB // 2
assert NB % 2 == 0
ARRIVING = [s + k * step for s, step, count in BATCHES for k in range(count)]
PLACE = [sum(x[2] for x in BATCHES[:b]) for b in range(NB)]
SHORT_BATCH = (8, 1, NE)
assert [f + 1 for f in PICKED_AT_START] == [8 + k for k in range(NE)] and (8, 1, 4) in BATCHES
NG = len(ARRIVING) - 1
assert sorted(ARRIVING + [f + 1 for f in PICKED]) == list(range(SLOTS))

TILES = BATCH // P
TP = 2
PHASES = TILES // TP
NS = TP * P
RING = 4
ROUNDS = TILES // RING
assert RING == 2 * TP
GT = P // 4
GROUPS = TP * GT
PITCH = 32
KZ = PAIRS // 3
M1, M2 = H1 // P, H2 // P

PIECES = NX0 + 4

U_Z, U_ZT, U_H1 = 0, 4, 6
USES = 8
V, S = 0, 1
EMPTIER = [S, V, S, V, V, V, S, S]
CHUNKS = [range(0, 2), range(2, 4), range(4, 6), range(6, 7), range(0), range(7, 8)]
assert len(CHUNKS) == NX
FIRST_TILE = [range(0), range(0), range(0), range(0, 2), range(2, 4), range(4, 6)]
FIRST_AT_START = [range(0)] * (NX0 - 3) + [range(0, 2), range(2, 4), range(4, 6)]
LAYER2 = [(m, k) for m in range(M2) for k in range(M1)]
LAYER2_PART = {1: LAYER2[0:3], 3: LAYER2[3:6], 5: LAYER2[6:]}


def batch(b, first):
    s0, step, count = BATCHES[b]
    skip = NE if first and s0 == SHORT_BATCH[0] else 0
    return s0 + skip, step, count - skip, PLACE[b] + skip


def is_first(n):
    return isinstance(n, int) and n == 0


def picks_before(n):
    return 0 if is_first(n) else n * NX + NE


def gathered(k, rounds):
    return 16 * (NG * rounds - (NE if k < TP else 0))


def even(batches):
    return [b for b in batches if b % 2 == 0]


def odd(batches):
    return [b for b in batches if b % 2 == 1]


def emptied(engine, uses):
    return sum(e == engine for e in EMPTIER[:uses])


def dlrm_tower(nc, dense, ids, tables, w1_in, b1_in, w2_in, b2_in, w3_in, out):
    with ExitStack() as ctx:
        def sb(name, shape, dt):
            return ctx.enter_context(nc.sbuf_tensor(name, shape, dt))

        def psum(name, shape):
            return ctx.enter_context(nc.psum_tensor(name, shape, F32))

        def sem(name):
            return ctx.enter_context(nc.semaphore(name))

        ident = sb("ident", [P, P], F32)
        ident16 = sb("ident16", [P, P], F16)
        vocab_i = sb("vocab_i", [P, VQ], I32)
        vocab_f = sb("vocab_f", [P, VQ], F32)
        ids_all = sb("ids_all", [P, TILES, len(VOCAB)], I32)
        ids16 = sb("ids16", [P, NX0, TILES], F16)
        ids_phase = sb("ids_phase", [P, NX0, TP], F16)
        ids_tile = sb("ids_tile", [P, RING, len(VOCAB)], I32)
        arrived = sb("arrived", [P, RING, NG + 1, D], F32)
        cols = sb("cols", [P, TP, P, PITCH], F32)
        with nc.sbuf_tensor("extra_b", [P, 2, VQ * D], F32R) as extra_b:
            pass
        pairs = sb("pairs", [GROUPS, 4, PAIRS], F32)
        h1_full = sb("h1_full", [P, M1, NS], F32)
        ids_wide = sb("ids_wide", [P, 2, NS], F16)
        onehot = sb("onehot", [P, 2, VQ, NS], F32R)
        table = sb("table", [P, NX, 2, VQ * D], F32R)
        h2 = sb("h2", [P, M2, NS], F32)
        w1 = sb("w1", [P, 2, 4, M1, P], F32R)
        w2 = sb("w2", [P, 2, M1, M2, P], F32R)
        prod = sb("prod", [P, COLS, GROUPS], F32)
        with nc.sbuf_tensor("extra_a", [P, 2, VQ * D], F32R) as extra_a:
            pass
        h1 = sb("h1", [P, 2, M1, NS], F32R)
        with nc.sbuf_tensor("raw", [P, 2, VQ * D], F32) as raw:
            pass
        pairs_t = sb("pairs_t", [P, 2, 3, NS], F32R)
        dense_t = sb("dense_t", [P, 2, NS], F32R)
        w3 = sb("w3", [P, M2], F32)
        b1 = sb("b1", [P, M1], F32)
        b2 = sb("b2", [P, M2], F32)
        warm = sb("warm", [P, 1], F32)
        y_all = sb("y_all", [P, TILES], F32)

        ps_ids = psum("ps_ids", [P, NS])
        ps_pick = psum("ps_pick", [P, M2, NS])
        ps_tr = psum("ps_tr", [P, 2, 4 * P])
        ps_prod = psum("ps_prod", [P, 4, 4, P])

        s_raw = [sem("s_raw0"), sem("s_raw1")]
        s_sum = sem("s_sum")
        s_hi = sem("s_hi")
        s_lo = sem("s_lo")
        s_ids = sem("s_ids")
        s_ids16 = sem("s_ids16")
        s_ident = sem("s_ident")
        s_ident0 = sem("s_ident0")
        s_const = sem("s_const")
        s_small = sem("s_small")
        s_zero = sem("s_zero")
        s_phase = sem("s_phase")
        s_idt = [sem(f"s_idt{k}") for k in range(RING)]
        s_dense = [sem(f"s_dense{k}") for k in range(RING)]
        s_rows = [sem(f"s_rows{k}") for k in range(RING)]
        s_wide_ps = sem("s_wide_ps")
        s_wide = sem("s_wide")
        s_onehot = sem("s_onehot")
        s_pick = sem("s_pick")
        s_picked = sem("s_picked")
        s_tr = sem("s_tr")
        s_cols = [sem("s_cols_v"), sem("s_cols_s")]
        s_prod_ps = sem("s_prod_ps")
        s_prod = [sem("s_prod_v"), sem("s_prod_s")]
        s_dense_hi = sem("s_dense_hi")
        s_dense_lo = sem("s_dense_lo")
        s_pairs_hi = sem("s_pairs_hi")
        s_h1_hi = sem("s_h1_hi")
        s_h1_lo = sem("s_h1_lo")
        s_tail_ps = sem("s_tail_ps")
        s_tail = [sem("s_tail_v"), sem("s_tail_s")]
        s_h2_ps = sem("s_h2_ps")
        s_h2 = sem("s_h2")
        s_y_ps = sem("s_y_ps")
        s_y = sem("s_y")
        s_turn = sem("s_turn")
        s_turn_pe = sem("s_turn_pe")
        s_out = sem("s_out")

        ids_rows = ids.rearrange("(p t) f -> p t f", t=TILES)
        dense_rows = dense.rearrange("(p t) d -> p t d", t=TILES)

        def table_part(i, part):
            home = table[:, i] if i < NX else (extra_a, extra_b)[i - NX]
            return home[0:VP, part, :]


        def empty_batch(engine, copy, me, n, t, b):
            s0, step, count, _ = batch(b, is_first(n))
            engine.wait_ge(s_tr, (n * TP + t) * NB + b + 1)
            dst = cols[:, t, :, s0:s0 + (count - 1) * step + 1:step].rearrange("d p s -> d s p")
            copy(dst, ps_tr[:, b % 2, 0:count * P].rearrange("d (s p) -> d s p", s=count)).then_inc(s_cols[me], 1)

        def empty_products(copy, t, h, done):
            b = 2 * (h % 2)
            g = t * GT + 8 * h
            for j in range(4):
                at = slice(32 * j, 32 * j + 32)
                for_j = ps_prod[at, b:b + 2, :, j * COLS:(j + 1) * COLS].rearrange("r b g c -> r (b g) c")
                last = copy(prod[at, :, g:g + 8].rearrange("r c g -> r g c"), for_j)
            last.then_inc(done, 1)

        def empty_pairs(copy, u, done):
            for c in range(8 * u, min(8 * u + 8, COLS)):
                half = slice(GROUPS * (c % 2), GROUPS * (c % 2) + GROUPS)
                bank = ps_prod[half, u % 4, (c % 8) // 2].rearrange("g (j r) -> g j r", j=4)
                start, n = PAIR_START[c], COLS - c
                last = copy(pairs[:, :, start:start + n], bank[:, :, c + 1:SLOTS])
            last.then_inc(done, 1)

        def pair_rows(u):
            thirds = range(2) if u == U_ZT else range(2, 3)
            bank = ps_prod[0:KZ, u % 4].rearrange("k a b -> k (a b)")[:, 0:len(thirds) * NS]
            return thirds, bank.rearrange("k (z j g) -> k z j g", z=len(thirds), j=4)

        def pair_part(part, thirds):
            dst = pairs_t[0:KZ, part, thirds[0]:thirds[-1] + 1, :]
            return dst.rearrange("k z (g j) -> k z j g", j=4)

        def piece(i):
            buf = raw[:, i % 2, :]
            if i < NX0:
                return buf[0:VP], table_part(i, HI), table_part(i, LO)
            if i < NX0 + 3:
                k0, count, rows = [(0, 1, P), (1, 2, KZ), (3, 1, KZ)][i - NX0]
                src = buf[0:rows, 0:count * H1].rearrange("p (k j m) -> p k m j", k=count, m=M1)
                return src, w1[0:rows, HI, k0:k0 + count], w1[0:rows, LO, k0:k0 + count]
            src = buf.rearrange("p (k j m) -> p k m j", k=M1, m=M2)
            return src, w2[:, HI], w2[:, LO]

        block = ctx.enter_context(nc.Block())

        @block.sync
        def _(sp):
            sp.dma_start(ids_all[:], ids_rows).then_inc(s_ids, 16)

            def load_tile(r, k, first):
                if not first:
                    sp.wait_ge(s_rows[k], gathered(k, r))
                sp.dma_start(ids_tile[:, k, :], ids_rows[:, bass.ds(r * RING + k, 1), :].rearrange("p a f -> p (a f)")
                             ).then_inc(s_idt[k], 16)
                if not first:
                    sp.wait_ge(s_tr, (r - 1) * RING * NB + (k + 1) * NB)
                sp.dma_start(arrived[:, k, 0, :], dense_rows[:, bass.ds(r * RING + k, 1), :].rearrange("p a d -> p (a d)")
                             ).then_inc(s_dense[k], 16)

            def load_piece(i):
                if i >= 2:
                    sp.wait_ge(s_lo, i - 1)
                buf = raw[:, i % 2, :]
                if i < NX0:
                    sp.dma_start(buf[0:VP], tables[(PICKED + PICKED_AT_START)[i]].rearrange("(p q) d -> p (q d)", q=VQ)
                                 ).then_inc(s_raw[i % 2], 16)
                elif i == NX0:
                    sp.dma_start(buf[:, 0:H1], w1_in[0:D, :]).then_inc(s_raw[i % 2], 16)
                    sp.dma_start(buf[:, H1:2 * H1], w1_in[D + PAIRS:, :]).then_inc(s_raw[i % 2], 16)
                elif i < NX0 + 3:
                    k0, count = [(0, 2), (2, 1)][i - NX0 - 1]
                    sp.dma_start(buf[0:KZ, 0:count * H1].rearrange("p (k h) -> p k h", k=count),
                                 w1_in[D + k0 * KZ:D + (k0 + count) * KZ, :].rearrange("(k p) h -> p k h", p=KZ)
                                 ).then_inc(s_raw[i % 2], 16)
                else:
                    sp.dma_start(buf, w2_in.rearrange("(p m) h -> p (m h)", m=M1)).then_inc(s_raw[i % 2], 16)

            load_tile(0, 0, True)
            load_piece(0)
            load_tile(0, 1, True)
            load_piece(1)
            load_tile(0, 2, True)
            load_tile(0, 3, True)
            for i in range(2, PIECES):
                load_piece(i)
            sp.dma_start(w3[:], w3_in.rearrange("(p m) o -> p (m o)", m=M2)).then_inc(s_small, 16)
            sp.dma_start(b1[:], b1_in.rearrange("(p m) -> p m", m=M1)).then_inc(s_small, 16)
            sp.dma_start(b2[:], b2_in.rearrange("(p m) -> p m", m=M2)).then_inc(s_small, 16)
            with sp.Fori(1, ROUNDS) as r:
                for k in range(RING):
                    load_tile(r, k, False)
            sp.wait_ge(s_y, PHASES)
            sp.dma_start(out.rearrange("(p t) o -> p (t o)", t=TILES), y_all[:]).then_inc(s_out, 16)
            sp.wait_ge(s_out, 16)

        @block.gpsimd
        def _(pool):
            nc.gpsimd.memset(ident[:], 0.0).then_inc(s_ident0, 1)
            pool.wait_ge(s_ident0, 1)
            nc.gpsimd.affine_select(out=ident[:], in_=ident[:], compare_op=ALU.not_equal, fill=1.0, base=0,
                                    pattern=[[-1, P]], channel_multiplier=1).then_inc(s_ident, 1)
            nc.gpsimd.iota(vocab_i[:], pattern=[[1, VQ]], base=0, channel_multiplier=VQ).then_inc(s_ident, 1)

            def gather_tile(r, k, first):
                pool.wait_ge(s_idt[k], 16 * (r + 1))
                if not first:
                    pool.wait_ge(s_tr, (r - 1) * RING * NB + (k + 1) * NB)
                    pool.sem_inc(s_turn, 1)
                for a in range(1, NG + 1):
                    f = ARRIVING[a] - 1
                    if first and k < TP and f in PICKED_AT_START:
                        continue
                    pool.indirect_dma_start(arrived[:, k, a, :], None, tables[f],
                                            bass.IndirectOffsetOnAxis(ids_tile[:, k, f:f + 1], 0)
                                            ).then_inc(s_rows[k], 16)

            for k in range(RING):
                gather_tile(0, k, True)
            with pool.Fori(1, ROUNDS) as r:
                for k in range(RING):
                    gather_tile(r, k, False)

        @block.tensor
        def _(pe):
            def spread_ids(n, i):
                if i == 0:
                    pe.wait_ge(s_phase, n + 1)
                if not (isinstance(n, int) and n == 0 and i == 0):
                    pe.wait_ge(s_wide, picks_before(n) + i)
                for t in range(TP):
                    last = nc.tensor.matmul(ps_ids[:, t * P:(t + 1) * P],
                                            ids_phase[:, i, t:t + 1].to_broadcast([P, P]), ident16[:],
                                            start=True, stop=True)
                last.then_inc(s_wide_ps, 1)

            def pick_rows(n, i, first):
                pe.wait_ge(s_onehot, (picks_before(n) + i + 1) * VQ)
                if not (first and i == 0):
                    pe.wait_ge(s_picked, picks_before(n) + i)
                if first:
                    pe.wait_ge(s_lo, i + 1)
                if i == 0 and not (isinstance(n, int) and n < 2):
                    pe.wait_ge(s_y, n - 1)
                for q in range(VQ):
                    for part in (HI, LO):
                        last = nc.tensor.matmul(ps_pick[:, 0, :], table_part(i, part)[:, q * D:(q + 1) * D],
                                                onehot[0:VP, i % 2, q, :],
                                                start=(q == 0 and part == 0), stop=(q == VQ - 1 and part == LO))
                last.then_inc(s_pick, 1)

            def transpose_batch(r, q, t, b):
                k = q * TP + t
                if b == 0:
                    pe.wait_ge(s_rows[k], gathered(k, r + 1))
                    pe.wait_ge(s_dense[k], 16 * (r + 1))
                if not (isinstance(r, int) and r == 0 and k == 0 and b < 2):
                    pe.wait_ge(s_cols[b % 2], (r * RING + k) * HB + b // 2)
                _, _, count, place = batch(b, is_first(r) and q == 0)
                for s in range(count):
                    last = nc.tensor.transpose(ps_tr[:, b % 2, s * P:(s + 1) * P],
                                               arrived[:, k, place + s, :], ident[:])
                last.then_inc(s_tr, 1)

            def multiply_tile(r, q, t, first):
                n = 2 * r + q
                for e in (V, S):
                    pe.wait_ge(s_cols[e], (n * TP + t + 1) * HB)
                if t == 0:
                    pe.wait_ge(s_picked, picks_before(n + 1))
                    if first:
                        pe.wait_ge(s_zero, 1)
                    else:
                        pe.wait_ge(s_tail[V], n * emptied(V, USES))
                        pe.wait_ge(s_tail[S], n * emptied(S, USES) - 1)
                for h in range(4):
                    if not first and t == 0 and h == 1:
                        pe.wait_ge(s_tail[S], n * emptied(S, USES))
                    if not (first and t == 0 and h < 2):
                        pe.wait_ge(s_prod[h % 2], (n * TP + t) * 2 + h // 2)
                    for g in range(8):
                        s = 4 * (8 * h + g)
                        dst = ps_prod[:, 2 * (h % 2) + g // 4, g % 4, 0:4 * COLS]
                        last = nc.tensor.matmul(dst, cols[:, t, s:s + 4, :].rearrange("d p s -> d (p s)"),
                                                cols[:, t, s:s + 4, 0:COLS], start=True, stop=True)
                    last.then_inc(s_prod_ps, 1)
                    if t == 1 and h == 1 and not first:
                        third_layer(n - 1)

            def layer(dst, weights, inputs, first=True, last=True):
                parts = [(HI, HI), (HI, LO), (LO, HI)]
                for k, (w, x) in enumerate(zip(weights, inputs)):
                    for a, b in parts:
                        done = nc.tensor.matmul(dst, w[:, a], x[:, b],
                                                start=(first and k == 0 and (a, b) == parts[0]),
                                                stop=(last and k == len(inputs) - 1 and (a, b) == parts[-1]))
                return done

            def second_layer(n, pairs_mk):
                for m, k in pairs_mk:
                    if m == 0:
                        pe.wait_ge(s_h1_lo, n * M1 + k + 1)
                    last = layer(ps_pick[:, m, :], [w2[:, :, k, m, :]], [h1[:, :, k, :]], k == 0, k == M1 - 1)
                if pairs_mk[-1] == LAYER2[-1]:
                    last.then_inc(s_h2_ps, 1)

            def tail(n, chunk):
                base = [n * emptied(e, USES) for e in (V, S)]
                for u in CHUNKS[chunk]:
                    bank = ps_prod[:, u % 4].rearrange("p a b -> p (a b)")
                    if u >= 4:
                        e = EMPTIER[u - 4]
                        pe.wait_ge(s_tail[e], base[e] + emptied(e, u - 3))
                    if u == U_Z:
                        pe.wait_ge(s_prod[0], (n + 1) * TP * 2)
                        pe.wait_ge(s_prod[1], (n + 1) * TP * 2)
                    if u == U_ZT:
                        pe.wait_ge(s_tail[V], base[V] + emptied(V, u))
                        pe.wait_ge(s_tail[S], base[S] + emptied(S, u))
                    if U_ZT <= u < U_H1:
                        pe.sem_inc(s_turn_pe, 1)
                    if u == U_H1:
                        pe.wait_ge(s_dense_lo, n + 1)
                        if isinstance(n, int) and n == 0:
                            pe.wait_ge(s_lo, PIECES)
                    if u < U_ZT:
                        for c in range(8 * u, min(8 * u + 8, COLS), 2):
                            last = nc.tensor.transpose(ps_prod[:, u % 4, (c % 8) // 2, :],
                                                       prod[:, c:c + 2, :].rearrange("r c g -> r (c g)"), ident[:])
                    elif u < U_H1:
                        thirds, dst = pair_rows(u)
                        for z, k in enumerate(thirds):
                            for j in range(4):
                                last = nc.tensor.transpose(dst[:, z, j, :], pairs[:, j, k * KZ:(k + 1) * KZ],
                                                           ident[0:GROUPS, 0:GROUPS])
                    else:
                        for z in range(2):
                            m = 2 * (u - U_H1) + z
                            dst = bank[:, z * NS:(z + 1) * NS]
                            layer(dst, [w1[:, :, 0, m, :]], [dense_t[:]], True, False)
                            for k in range(3):
                                if m == 0 and k in (0, 2):
                                    pe.wait_ge(s_tail[V], base[V] + emptied(V, U_ZT + 1 + k // 2))
                                last = layer(dst, [w1[0:KZ, :, k + 1, m, :]], [pairs_t[0:KZ, :, k, :]], False, k == 2)
                    last.then_inc(s_tail_ps, 1)

            def third_layer(n):
                pe.wait_ge(s_h2, n + 1)
                for t in range(TP):
                    for k in range(M2):
                        last = nc.tensor.matmul(ps_pick[:, 0, t:t + 1], h2[:, k, t * P:(t + 1) * P], w3[:, k:k + 1],
                                                start=(k == 0), stop=(k == M2 - 1))
                last.then_inc(s_y_ps, 1)

            def picks(r, q, first):
                n = 2 * r + q
                tables_now = NX0 if first else NX
                for i in range(tables_now):
                    if i + 2 < tables_now:
                        spread_ids(n, i + 2)
                    pick_rows(n, i, first)
                    for b in (FIRST_AT_START if first else FIRST_TILE)[i]:
                        transpose_batch(r, q, 0, b)
                    if not first:
                        tail(n - 1, i)

            def tiles(r, q, first, last):
                n = 2 * r + q
                if not last:
                    spread_ids(n + 1, 0)
                multiply_tile(r, q, 0, first)
                for b in range(NB):
                    transpose_batch(r, q, 1, b)
                    if not first and b in LAYER2_PART:
                        second_layer(n - 1, LAYER2_PART[b])
                if not last:
                    spread_ids(n + 1, 1)
                multiply_tile(r, q, 1, first)

            pe.wait_ge(s_const, 2)
            spread_ids(0, 0)
            spread_ids(0, 1)
            picks(0, 0, True)
            tiles(0, 0, True, False)
            pe.wait_ge(s_small, 16 * 3)
            picks(0, 1, False)
            with pe.Fori(1, ROUNDS) as r:
                tiles(r - 1, 1, False, False)
                picks(r, 0, False)
                tiles(r, 0, False, False)
                picks(r, 1, False)
            tiles(ROUNDS - 1, 1, False, True)
            for chunk in range(len(CHUNKS)):
                tail(PHASES - 1, chunk)
            second_layer(PHASES - 1, LAYER2)
            third_layer(PHASES - 1)

        @block.vector
        def _(dve):
            copy = nc.vector.tensor_copy

            def one_hot(n, i, first):
                for q in range(VQ):
                    if q == 0:
                        dve.wait_ge(s_wide, picks_before(n) + i + 1)
                        if not (first and i < 2):
                            dve.wait_ge(s_pick, picks_before(n) + i - 1)
                    nc.vector.tensor_scalar(onehot[0:VP, i % 2, q, :], ids_wide[0:VP, i % 2, :],
                                            vocab_f[0:VP, q:q + 1], None, ALU.is_equal).then_inc(s_onehot, 1)

            def split_piece(i):
                src, hi, lo = piece(i)
                if i == NX0:
                    dve.wait_ge(s_raw[i % 2], 16 * (i // 2 + 2))
                    nc.vector.tensor_tensor(raw[:, i % 2, 0:H1], raw[:, i % 2, 0:H1], raw[:, i % 2, H1:2 * H1],
                                            ALU.add).then_inc(s_sum, 1)
                dve.wait_ge(s_hi, i + 1)
                nc.vector.tensor_tensor(lo, src, hi.bitcast(F32), ALU.subtract).then_inc(s_lo, 1)

            def empty_tail(n, chunk):
                for u in CHUNKS[chunk]:
                    bank = ps_prod[:, u % 4].rearrange("p g c -> p (g c)")
                    if u >= U_H1:
                        for m in range(2 * (u - U_H1), 2 * (u - U_H1) + 2):
                            dve.wait_ge(s_h1_hi, n * M1 + m + 1)
                            nc.vector.tensor_tensor(h1[:, LO, m, :], h1_full[:, m, :], h1[:, HI, m, :].bitcast(F32),
                                                    ALU.subtract).then_inc(s_h1_lo, 1)
                    if EMPTIER[u] != V:
                        continue
                    dve.wait_ge(s_tail_ps, n * USES + u + 1)
                    if u < U_ZT:
                        empty_pairs(copy, u, s_tail[V])
                    else:
                        thirds, src = pair_rows(u)
                        dve.wait_ge(s_pairs_hi, n * 2 + (u - U_ZT) + 1)
                        for z, k in enumerate(thirds):
                            last = nc.vector.tensor_tensor(pair_part(LO, [k])[:, 0], src[:, z],
                                                           pair_part(HI, [k])[:, 0].bitcast(F32), ALU.subtract)
                        last.then_inc(s_tail[V], 1)

            def empty_results(n):
                dve.wait_ge(s_y_ps, n + 1)
                copy(y_all[:, bass.ds(n * TP, TP)], ps_pick[:, 0, 0:TP]).then_inc(s_y, 1)

            def stage_ids(n):
                if not (isinstance(n, int) and n == 0):
                    dve.wait_ge(s_wide_ps, picks_before(n))
                copy(ids_phase[:], ids16[:, :, bass.ds(n * TP, TP)]).then_inc(s_phase, 1)

            def picks(n, first):
                tables_now = NX0 if first else NX
                for i in range(tables_now):
                    if first and i > 0:
                        split_piece(i + 1)
                    if i + 2 < tables_now and i not in (1, 2):
                        one_hot(n, i + 2, first)
                    for b in even((FIRST_AT_START if first else FIRST_TILE)[i]):
                        empty_batch(dve, copy, V, n, 0, b)
                    if not first and i < NX - 1:
                        empty_tail(n - 1, i)
                    if i + 2 < tables_now and i in (1, 2):
                        one_hot(n, i + 2, first)

            def tiles(n, first, last):
                if not last:
                    stage_ids(n + 1)
                if not first:
                    empty_tail(n - 1, NX - 1)
                if first:
                    split_piece(NX0 + 1)
                for t in range(TP):
                    for h in (0, 2):
                        dve.wait_ge(s_prod_ps, n * TP * 4 + 4 * t + h + 1)
                        empty_products(copy, t, h, s_prod[0])
                        if first and t == 0:
                            split_piece(NX0 + 2 + h // 2)
                        if not last and h == 0:
                            one_hot(n + 1, t, False)
                        if t == 0 and h == 2:
                            for b in even(range(NB)):
                                empty_batch(dve, copy, V, n, 1, b)
                if not first:
                    empty_results(n - 1)
                dve.wait_ge(s_dense_hi, n + 1)
                nc.vector.tensor_tensor(dense_t[:, LO].rearrange("d (t p) -> d t p", t=TP), cols[:, :, :, 0],
                                        dense_t[:, HI].bitcast(F32).rearrange("d (t p) -> d t p", t=TP),
                                        ALU.subtract).then_inc(s_dense_lo, 1)

            dve.wait_ge(s_ident, 2)
            copy(ident16[:], ident[:]).then_inc(s_const, 1)
            nc.vector.memset(cols[:, :, :, SLOTS:PITCH], 0.0).then_inc(s_zero, 1)
            copy(vocab_f[:], vocab_i[:]).then_inc(s_const, 1)
            dve.wait_ge(s_ids, 16)
            for i, f in enumerate(PICKED + PICKED_AT_START):
                copy(ids16[:, i, :], ids_all[:, :, f]).then_inc(s_ids16, 1)
            dve.wait_ge(s_ids16, NX0)
            dve.wait_ge(s_const, 2)
            stage_ids(0)
            split_piece(0)
            one_hot(0, 0, True)
            split_piece(1)
            one_hot(0, 1, True)
            picks(0, True)
            tiles(0, True, False)
            picks(1, False)
            with dve.Fori(2, PHASES) as n:
                tiles(n - 1, False, False)
                picks(n, False)
            tiles(PHASES - 1, False, True)
            for chunk in range(len(CHUNKS)):
                empty_tail(PHASES - 1, chunk)
            empty_results(PHASES - 1)

        @block.scalar
        def _(act):
            copy = nc.scalar.copy

            def widen(n, i, first):
                act.wait_ge(s_wide_ps, picks_before(n) + i + 1)
                if not (first and i < 2):
                    act.wait_ge(s_onehot, (picks_before(n) + i - 1) * VQ)
                copy(ids_wide[:, i % 2, :], ps_ids[:]).then_inc(s_wide, 1)

            def split_piece(i):
                src, hi, lo = piece(i)
                if i == NX0:
                    act.wait_ge(s_sum, 1)
                else:
                    act.wait_ge(s_raw[i % 2], 16 * (i // 2 + 1 + (i > NX0 and (i - NX0) % 2 == 0)))
                copy(hi, src).then_inc(s_hi, 1)

            def empty_tail(n, chunk):
                for u in CHUNKS[chunk]:
                    bank = ps_prod[:, u % 4].rearrange("p g c -> p (g c)")
                    if U_ZT <= u < U_H1:
                        thirds, src = pair_rows(u)
                        act.wait_ge(s_tail_ps, n * USES + u + 1)
                        for z, k in enumerate(thirds):
                            last = copy(pair_part(HI, [k])[:, 0], src[:, z])
                        last.then_inc(s_pairs_hi, 1)
                    if EMPTIER[u] != S:
                        continue
                    act.wait_ge(s_tail_ps, n * USES + u + 1)
                    if u < U_ZT:
                        empty_pairs(copy, u, s_tail[S])
                    else:
                        tiles = range(2 * (u - U_H1), 2 * (u - U_H1) + 2)
                        if is_first(n):
                            act.wait_ge(s_small, 16 * 3)
                        for z, m in enumerate(tiles):
                            last = nc.scalar.activation(h1_full[:, m, :], bank[:, z * NS:(z + 1) * NS], ACT.Relu,
                                                        bias=b1[:, m:m + 1])
                        last.then_inc(s_tail[S], 1)
                        act.wait_ge(s_tail[S], n * emptied(S, USES) + emptied(S, u + 1))
                        for m in tiles:
                            copy(h1[:, HI, m, :], h1_full[:, m, :]).then_inc(s_h1_hi, 1)

            def rectify_h2(n):
                act.wait_ge(s_h2_ps, n + 1)
                for m in range(M2):
                    last = nc.scalar.activation(h2[:, m, :], ps_pick[:, m, :], ACT.Relu, bias=b2[:, m:m + 1])
                last.then_inc(s_h2, 1)

            def picks(n, first):
                tables_now = NX0 if first else NX
                for i in range(tables_now):
                    if first and i > 0:
                        split_piece(i + 1)
                    if i + 2 < tables_now:
                        widen(n, i + 2, first)
                    act.wait_ge(s_pick, picks_before(n) + i + 1)
                    copy(cols[:, :, :, (PICKED + PICKED_AT_START)[i] + 1], ps_pick[:, 0, :].rearrange("d (t p) -> d t p", t=TP)
                         ).then_inc(s_picked, 1)
                    for b in odd((FIRST_AT_START if first else FIRST_TILE)[i]):
                        empty_batch(act, copy, S, n, 0, b)
                    if not first:
                        empty_tail(n - 1, i)

            def tiles(n, first, last):
                for t in range(TP):
                    if not last:
                        widen(n + 1, t, False)
                    if first and t == 0:
                        split_piece(NX0 + 1)
                    for h in (1, 3):
                        act.wait_ge(s_prod_ps, n * TP * 4 + 4 * t + h + 1)
                        empty_products(copy, t, h, s_prod[1])
                        if first and t == 0:
                            split_piece(NX0 + 2 + h // 2)
                    if t == 0:
                        for b in odd(range(NB)):
                            empty_batch(act, copy, S, n, 1, b)
                        if not first:
                            rectify_h2(n - 1)
                if first:
                    act.wait_ge(s_lo, PIECES)
                copy(dense_t[:, HI].rearrange("d (t p) -> d t p", t=TP), cols[:, :, :, 0]).then_inc(s_dense_hi, 1)

            act.wait_ge(s_ident, 2)
            nc.scalar.activation(warm[:], ident[:, 0:1], ACT.Relu)
            split_piece(0)
            widen(0, 0, True)
            split_piece(1)
            widen(0, 1, True)
            picks(0, True)
            tiles(0, True, False)
            picks(1, False)
            with act.Fori(2, PHASES) as n:
                tiles(n - 1, False, False)
                picks(n, False)
            tiles(PHASES - 1, False, True)
            for chunk in range(len(CHUNKS)):
                empty_tail(PHASES - 1, chunk)
            rectify_h2(PHASES - 1)



def kernel(**inputs):
    import numpy as _np
    import concourse.bacc as _bacc
    from concourse import mybir as _mybir
    from concourse.bass_utils import run_bass_kernel_spmd as _run

    nc = _bacc.Bacc("TRN2", target_bir_lowering=False, num_devices=1)
    arrays, args = {}, {}
    names = ["r_dense_features", "ids"] + [f"tbl_{f}" for f in range(len(VOCAB))]
    for name in names + ["W_top1", "b_top1", "W_top2", "b_top2", "W_top3"]:
        a = _np.ascontiguousarray(inputs[name])
        arrays[f"in_{name}_dram"] = a
        args[name] = nc.dram_tensor(f"in_{name}_dram", a.shape, _mybir.dt.from_np(a.dtype), kind="ExternalInput").ap()
    out = nc.dram_tensor("out_0_dram", (BATCH, 1), F32, kind="ExternalOutput").ap()
    dlrm_tower(nc, args["r_dense_features"], args["ids"], [args[f"tbl_{f}"] for f in range(len(VOCAB))],
               args["W_top1"], args["b_top1"], args["W_top2"], args["b_top2"], args["W_top3"], out)
    r = _run(nc, [arrays], core_ids=[0])
    return r.results[0]["out_0_dram"]
```
